# Optimizing a Trainium2 kernel written in Bass

```python
import numpy as np
import jax
import jax.numpy as jnp

def _softmax(x, axis=-1):
    return jax.nn.softmax(x, axis=axis)

def _gelu(x):
    return jax.nn.gelu(x, approximate=True)

def _silu(x):
    return jax.nn.silu(x)

def _sigmoid(x):
    return jax.nn.sigmoid(x)

def _layernorm(x, axis=-1, eps=1e-05):
    m = jnp.mean(x, axis=axis, keepdims=True)
    v = jnp.var(x, axis=axis, keepdims=True)
    return (x - m) / jnp.sqrt(v + eps)

def _scatter_add(tgt, idx, src, axis=0):
    return tgt.at[idx].add(src)

def _segment_sum(src, seg, n):
    return jax.ops.segment_sum(src, seg, n)
kernel_name = 'mk_seq_preln_d1_jaxref_r8_29f8b2'

def setup_inputs(seed: int=0):
    np.random.seed(seed)
    _w = jnp.asarray

    def _L0_attn_setup():
        import jax, jax.numpy as jnp
        import numpy as np
        D_MODEL, D_STATE, D_CONV, EXPAND = (128, 16, 4, 2)
        D_INNER = EXPAND * D_MODEL
        BATCH, SEQ = (2, 256)

        def _forward(x, in_proj_w, conv_w, conv_b, dt_w, dt_b, A_log, D, B_w, C_w, out_w):
            xz = x @ in_proj_w.T
            xc, z = jnp.split(xz, 2, axis=-1)
            h = jnp.transpose(xc, (0, 2, 1))
            h = jnp.pad(h, ((0, 0), (0, 0), (D_CONV - 1, 0)))
            h = jax.lax.conv_general_dilated(h, conv_w, (1,), 'VALID', dimension_numbers=('NCH', 'OIH', 'NCH'))
            h = h + conv_b[None, :, None]
            u = jnp.transpose(h, (0, 2, 1))
            dt = jnp.clip(jax.nn.sigmoid(u @ dt_w.T + dt_b), 0.0001, 1.0)
            A = -jnp.exp(A_log)
            Bm = u @ B_w.T
            Cm = u @ C_w.T
            u_t = jnp.transpose(u, (1, 0, 2))
            dt_t = jnp.transpose(dt, (1, 0, 2))
            B_t = jnp.transpose(Bm, (1, 0, 2))
            C_t = jnp.transpose(Cm, (1, 0, 2))

            def step(state, inp):
                ut, dtt, bt, ct = inp
                dA = jnp.exp(jnp.clip(dtt[:, :, None] * A, -5.0, 5.0))
                dB = dtt[:, :, None] * bt[:, None, :] * ut[:, :, None]
                state = dA * state + dB + 1e-06
                y = jnp.sum(state * ct[:, None, :], axis=-1) + D * ut
                return (state, y)
            state0 = jnp.zeros((x.shape[0], D_INNER, D_STATE), x.dtype)
            _, ys = jax.lax.scan(step, state0, (u_t, dt_t, B_t, C_t))
            y = jnp.transpose(ys, (1, 0, 2))
            y = y * jax.nn.silu(z)
            return y @ out_w.T
        key = jax.random.key(seed)
        ks = jax.random.split(key, 10)
        inv = lambda n: 1.0 / np.sqrt(n)
        return {'x': jax.random.normal(ks[0], (BATCH, SEQ, D_MODEL), jnp.float32), 'in_proj_w': jax.random.uniform(ks[1], (2 * D_INNER, D_MODEL), jnp.float32, -inv(D_MODEL), inv(D_MODEL)), 'conv_w': jax.random.uniform(ks[2], (D_INNER, D_INNER, D_CONV), jnp.float32, -inv(D_INNER * D_CONV), inv(D_INNER * D_CONV)), 'conv_b': jax.random.uniform(ks[3], (D_INNER,), jnp.float32, -inv(D_INNER * D_CONV), inv(D_INNER * D_CONV)), 'dt_w': jax.random.uniform(ks[4], (D_INNER, D_INNER), jnp.float32, -inv(D_INNER), inv(D_INNER)), 'dt_b': jax.random.uniform(ks[5], (D_INNER,), jnp.float32, -inv(D_INNER), inv(D_INNER)), 'A_log': jax.random.normal(ks[6], (D_INNER, D_STATE), jnp.float32) * 0.01, 'D': jnp.ones((D_INNER,), jnp.float32), 'B_w': jax.random.uniform(ks[7], (D_STATE, D_INNER), jnp.float32, -inv(D_INNER), inv(D_INNER)), 'C_w': jax.random.uniform(ks[8], (D_STATE, D_INNER), jnp.float32, -inv(D_INNER), inv(D_INNER)), 'out_w': jax.random.uniform(ks[9], (D_MODEL, D_INNER), jnp.float32, -inv(D_INNER), inv(D_INNER))}
    _L0_attn_in = _L0_attn_setup()

    def _L0_ffn_setup():
        import jax, jax.numpy as jnp
        import numpy as np
        H = 128
        I = 256
        E = 8
        TOP_K = 2
        NUM_SHARED = 1
        key = jax.random.key(seed)
        ks = jax.random.split(key, 9)
        s = 0.02
        x = jax.random.normal(ks[0], (2, 256, H), dtype=jnp.float32)
        sg_w = jax.random.normal(ks[1], (I, H), dtype=jnp.float32) * s
        su_w = jax.random.normal(ks[2], (I, H), dtype=jnp.float32) * s
        sd_w = jax.random.normal(ks[3], (H, I), dtype=jnp.float32) * s
        router_w = jax.random.normal(ks[4], (E, H), dtype=jnp.float32) * s
        routing_bias = jnp.zeros((E,), dtype=jnp.float32)
        wg = jax.random.normal(ks[5], (E, I, H), dtype=jnp.float32) * s
        wu = jax.random.normal(ks[6], (E, I, H), dtype=jnp.float32) * s
        wd = jax.random.normal(ks[7], (E, H, I), dtype=jnp.float32) * s
        return {'x': x, 'sg_w': sg_w, 'su_w': su_w, 'sd_w': sd_w, 'router_w': router_w, 'routing_bias': routing_bias, 'wg': wg, 'wu': wu, 'wd': wd}
    _L0_ffn_in = _L0_ffn_setup()
    _d = {'L0_attn_x': _L0_attn_in['x'], 'L0_attn_in_proj_w': _L0_attn_in['in_proj_w'], 'L0_attn_conv_w': _L0_attn_in['conv_w'], 'L0_attn_conv_b': _L0_attn_in['conv_b'], 'L0_attn_dt_w': _L0_attn_in['dt_w'], 'L0_attn_dt_b': _L0_attn_in['dt_b'], 'L0_attn_A_log': _L0_attn_in['A_log'], 'L0_attn_D': _L0_attn_in['D'], 'L0_attn_B_w': _L0_attn_in['B_w'], 'L0_attn_C_w': _L0_attn_in['C_w'], 'L0_attn_out_w': _L0_attn_in['out_w'], 'L0_ffn_sg_w': _L0_ffn_in['sg_w'], 'L0_ffn_su_w': _L0_ffn_in['su_w'], 'L0_ffn_sd_w': _L0_ffn_in['sd_w'], 'L0_ffn_router_w': _L0_ffn_in['router_w'], 'L0_ffn_routing_bias': _L0_ffn_in['routing_bias'], 'L0_ffn_wg': _L0_ffn_in['wg'], 'L0_ffn_wu': _L0_ffn_in['wu'], 'L0_ffn_wd': _L0_ffn_in['wd']}
    _x0 = _d['L0_attn_x']
    _d['L0_attn_x'] = jax.random.normal(jax.random.fold_in(jax.random.key(seed), 1), (32, 256, 128), dtype=_x0.dtype)
    del _x0
    return _d

def reference(L0_attn_x, L0_attn_in_proj_w, L0_attn_conv_w, L0_attn_conv_b, L0_attn_dt_w, L0_attn_dt_b, L0_attn_A_log, L0_attn_D, L0_attn_B_w, L0_attn_C_w, L0_attn_out_w, L0_ffn_sg_w, L0_ffn_su_w, L0_ffn_sd_w, L0_ffn_router_w, L0_ffn_routing_bias, L0_ffn_wg, L0_ffn_wu, L0_ffn_wd):

    def _L0_attn_ref(x, in_proj_w, conv_w, conv_b, dt_w, dt_b, A_log, D, B_w, C_w, out_w):
        import jax, jax.numpy as jnp
        import numpy as np
        D_MODEL, D_STATE, D_CONV, EXPAND = (128, 16, 4, 2)
        D_INNER = EXPAND * D_MODEL
        BATCH, SEQ = (2, 256)

        def _forward(x, in_proj_w, conv_w, conv_b, dt_w, dt_b, A_log, D, B_w, C_w, out_w):
            xz = x @ in_proj_w.T
            xc, z = jnp.split(xz, 2, axis=-1)
            h = jnp.transpose(xc, (0, 2, 1))
            h = jnp.pad(h, ((0, 0), (0, 0), (D_CONV - 1, 0)))
            h = jax.lax.conv_general_dilated(h, conv_w, (1,), 'VALID', dimension_numbers=('NCH', 'OIH', 'NCH'))
            h = h + conv_b[None, :, None]
            u = jnp.transpose(h, (0, 2, 1))
            dt = jnp.clip(jax.nn.sigmoid(u @ dt_w.T + dt_b), 0.0001, 1.0)
            A = -jnp.exp(A_log)
            Bm = u @ B_w.T
            Cm = u @ C_w.T
            u_t = jnp.transpose(u, (1, 0, 2))
            dt_t = jnp.transpose(dt, (1, 0, 2))
            B_t = jnp.transpose(Bm, (1, 0, 2))
            C_t = jnp.transpose(Cm, (1, 0, 2))

            def step(state, inp):
                ut, dtt, bt, ct = inp
                dA = jnp.exp(jnp.clip(dtt[:, :, None] * A, -5.0, 5.0))
                dB = dtt[:, :, None] * bt[:, None, :] * ut[:, :, None]
                state = dA * state + dB + 1e-06
                y = jnp.sum(state * ct[:, None, :], axis=-1) + D * ut
                return (state, y)
            state0 = jnp.zeros((x.shape[0], D_INNER, D_STATE), x.dtype)
            _, ys = jax.lax.scan(step, state0, (u_t, dt_t, B_t, C_t))
            y = jnp.transpose(ys, (1, 0, 2))
            y = y * jax.nn.silu(z)
            return y @ out_w.T
        return _forward(x, in_proj_w, conv_w, conv_b, dt_w, dt_b, A_log, D, B_w, C_w, out_w)

    def _L0_ffn_ref(x, sg_w, su_w, sd_w, router_w, routing_bias, wg, wu, wd):
        import jax, jax.numpy as jnp
        import numpy as np
        H = 128
        I = 256
        E = 8
        TOP_K = 2
        NUM_SHARED = 1
        orig_shape = x.shape
        xt = x.reshape(-1, H)
        T = xt.shape[0]
        shared = jax.nn.silu(xt @ sg_w.T) * (xt @ su_w.T) @ sd_w.T
        shared = shared / NUM_SHARED
        logits = xt @ router_w.T + routing_bias
        probs = jax.nn.sigmoid(logits)
        topk_p, topk_idx = jax.lax.top_k(probs, TOP_K)
        topk_p = topk_p / jnp.sum(topk_p, axis=-1, keepdims=True)
        w = jnp.zeros((T, E), dtype=xt.dtype)
        w = w.at[jnp.arange(T)[:, None], topk_idx].add(topk_p)
        g = jnp.einsum('th,eih->tei', xt, wg)
        u = jnp.einsum('th,eih->tei', xt, wu)
        h = jax.nn.silu(g) * u
        y = jnp.einsum('tei,ehi->teh', h, wd)
        routed = jnp.einsum('te,teh->th', w, y)
        return (shared + routed).reshape(orig_shape)
    x = L0_attn_x
    x = x + _L0_attn_ref(_layernorm(x, axis=-1), L0_attn_in_proj_w, L0_attn_conv_w, L0_attn_conv_b, L0_attn_dt_w, L0_attn_dt_b, L0_attn_A_log, L0_attn_D, L0_attn_B_w, L0_attn_C_w, L0_attn_out_w)
    x = x + _L0_ffn_ref(_layernorm(x, axis=-1), L0_ffn_sg_w, L0_ffn_su_w, L0_ffn_sd_w, L0_ffn_router_w, L0_ffn_routing_bias, L0_ffn_wg, L0_ffn_wu, L0_ffn_wd)
    return x

_drawn_inputs = setup_inputs


def setup_inputs(seed=0):
    import zlib

    import numpy as np

    out = dict(_drawn_inputs(seed))
    spreads = {'L0_attn_D': (1.0, 0.6), 'L0_ffn_routing_bias': (0.0, 0.8)}
    factors = {'L0_attn_conv_b': 8.0,
     'L0_attn_dt_w': 8.0,
     'L0_attn_dt_b': 8.0,
     'L0_attn_A_log': 8.0,
     'L0_attn_B_w': 8.0,
     'L0_attn_C_w': 8.0,
     'L0_ffn_sg_w': 6.761,
     'L0_ffn_su_w': 6.635,
     'L0_ffn_sd_w': 6.593,
     'L0_ffn_router_w': 8.0,
     'L0_ffn_wg': 8.0,
     'L0_ffn_wu': 8.0,
     'L0_ffn_wd': 8.0}
    for name, (base, spread) in spreads.items():
        noise = np.random.default_rng([zlib.crc32(name.encode()), seed]).standard_normal(out[name].shape)
        drawn = base * np.exp(spread * noise) if base else spread * noise
        out[name] = jnp.asarray(drawn.astype(out[name].dtype))
    for name, factor in factors.items():
        out[name] = (out[name] * factor).astype(out[name].dtype)
    return out
```

```python
from contextlib import ExitStack

import numpy as np
import concourse.bass as bass
from concourse import mybir

F32 = mybir.dt.float32
ALU = mybir.AluOpType
ACT = mybir.ActivationFunctionType
AX = mybir.AxisListType

P = 128
DM = 128
CH = 256
HALVES = CH // P
NS = 16
TAPS = 4
SEQ = 256
TOKENS = 32 * SEQ
TOK = 512
SPG = TOK // SEQ
CHUNKS = TOK // P
PAIRS = CHUNKS // 2
GROUPS = TOKENS // TOK
SLOTS = NS
EXPERTS = 8
NETS = EXPERTS + 1
HID = 256
UNITS = 2 * NETS
LN_EPS = 1e-5
STATE_EPS = 1e-6
CLIP = 5.0
DT_MIN = 1e-4
DA_RING = 8
DB_RING = 4
EXP_SLOTS = {2: 4, 6: 8, 10: 12, 14: 0}
LEAD = 2
FIRST_UNIT_SLOT = 5
ROUTE_STEPS = 15


def unit_slot(i):
    return FIRST_UNIT_SLOT + i * (SLOTS - FIRST_UNIT_SLOT) // UNITS


UNITS_OF_SLOT = {s: [i for i in range(UNITS) if unit_slot(i) == s] for s in range(SLOTS)}


def at_least(eng, sem, value):
    if isinstance(value, int) and value <= 0:
        return
    eng.wait_ge(sem, value)


def wait_apart(eng, sem, value, passed):
    if isinstance(value, int) and value <= 0:
        return
    eng.wait_ge(sem, value)
    if not isinstance(value, int):
        eng.sem_inc(passed, 1)


def transfers(g, odd):
    return 8 * (g - odd) + 16


def run_steps(eng, step):
    step(-1, 1, False, True, False)
    step(0, 0, True, True, False)
    step(1, 1, True, True, True)
    with eng.Fori(0, GROUPS // 2 - 2) as pair:
        step(2 * pair + 2, 0, True, True, True)
        step(2 * pair + 3, 1, True, True, True)
    step(GROUPS - 2, 0, True, True, True)
    step(GROUPS - 1, 1, True, False, True)
    step(GROUPS, 0, False, False, True)


def build(nc, x, w_in, w_z, w_conv, w_dt, w_bc, w_out, chan, w_router, b_router,
          w_gate, w_up, w_down, out):
    x_v = x.rearrange("(g c p) d -> g p c d", c=CHUNKS, p=P)
    out_v = out.rearrange("(g c p) d -> g p c d", c=CHUNKS, p=P)

    ctx = ExitStack()
    with ctx:
        def sb(name, shape):
            return ctx.enter_context(nc.sbuf_tensor(name, shape, F32))

        def pb(name, shape):
            return ctx.enter_context(nc.psum_tensor(name, shape, F32))

        def sem(name):
            return ctx.enter_context(nc.semaphore(name))

        ident = sb("ident", [P, P])
        win_sb = sb("win_sb", [P, HALVES, DM])
        wz_sb = sb("wz_sb", [P, CH])
        wconv_sb = sb("wconv_sb", [P, HALVES, TAPS, CH])
        wtap = sb("wtap", [P, TAPS, CH])
        wdt_sb = sb("wdt_sb", [P, HALVES, CH])
        wbc_sb = sb("wbc_sb", [P, HALVES, 2 * NS])
        wout_sb = sb("wout_sb", [P, HALVES, DM])
        chan_sb = sb("chan_sb", [P, HALVES, NS + 3])
        A_sb = sb("A_sb", [P, HALVES, NS])
        wr_sb = sb("wr_sb", [P, EXPERTS])
        br_sb = sb("br_sb", [1, EXPERTS])
        ones = sb("ones", [1, P])
        rank = sb("rank", [P, EXPERTS])
        neg_half = sb("neg_half", [P, CHUNKS])
        wg_sb = sb("wg_sb", [P, NETS, HID])
        wu_sb = sb("wu_sb", [P, NETS, HID])
        wd_sb = sb("wd_sb", [P, NETS, 2, DM])

        x_sb = sb("x_sb", [P, 2, CHUNKS, DM])
        stats1 = sb("stats1", [P, CHUNKS, 6])
        mv1 = sb("mv1", [P, CHUNKS, 2])
        rstd1 = sb("rstd1", [P, CHUNKS])
        xn = sb("xn", [P, CHUNKS, DM])
        xnT = sb("xnT", [P, SPG, TAPS - 1 + SEQ])
        u_sb = sb("u_sb", [P, 2, HALVES, TOK])
        dtl = sb("dtl", [P, HALVES, TOK])
        dt_sb = sb("dt_sb", [P, 2, HALVES, TOK])
        w_sb = sb("w_sb", [P, HALVES, TOK])
        wT = sb("wT", [P, 2, CHUNKS, CH])
        bc = sb("bc", [P, 2, CHUNKS, 2 * NS])
        sz = sb("sz", [P, 2, HALVES, TOK])
        dA = sb("dA", [P, DA_RING, HALVES, TOK])
        dBT = sb("dBT", [P, DB_RING, CHUNKS, CH])
        h = sb("h", [P, 2, HALVES, TOK])
        yT = sb("yT", [P, 2, CHUNKS, CH])
        yd = sb("yd", [P, HALVES, TOK])
        yz = sb("yz", [P, HALVES, TOK])
        x1 = sb("x1", [P, 2, CHUNKS, DM])
        stats2 = sb("stats2", [P, CHUNKS, 6])
        mv2 = sb("mv2", [P, CHUNKS, 2])
        rstd2 = sb("rstd2", [P, CHUNKS])
        xn2 = sb("xn2", [P, CHUNKS, DM])
        xn2T = sb("xn2T", [P, TOK])
        logit = sb("logit", [P, CHUNKS, EXPERTS])
        prob = sb("prob", [P, CHUNKS, EXPERTS])
        hit = [sb(f"hit{j}", [P, CHUNKS, EXPERTS]) for j in range(2)]
        key = sb("key", [P, CHUNKS, EXPERTS])
        rest = sb("rest", [P, CHUNKS, EXPERTS])
        top = [sb(f"top{j}", [P, CHUNKS]) for j in range(2)]
        win = sb("win", [P, CHUNKS])
        share = sb("share", [P, CHUNKS])
        route = sb("route", [P, CHUNKS, EXPERTS])
        sg = sb("sg", [P, 2, TOK])
        hm = sb("hm", [P, 2, 2, TOK])

        p_dB = [pb(f"p_dB{i}", [P, TOK]) for i in range(HALVES)]
        p_hT = [pb(f"p_hT{i}", [P, 2, CH]) for i in range(PAIRS)]
        p_gate = pb("p_gate", [P, TOK])
        p_up = pb("p_up", [P, TOK])
        p_down = pb("p_down", [P, CHUNKS, DM])
        p_misc = pb("p_misc", [P, TOK])

        mixer_weights = sem("mixer_weights")
        expert_weights = sem("expert_weights")
        consts = sem("consts")
        pool_passed = sem("pool_passed")
        dve_passed = sem("dve_passed")
        ident_set = sem("ident_set")
        a_exp = sem("a_exp")
        a_ready = sem("a_ready")
        tap_in_psum = sem("tap_in_psum")
        tap_ready = sem("tap_ready")
        x_loaded = [sem(f"x_loaded{j}") for j in range(2)]
        res_loaded = [sem(f"res_loaded{j}") for j in range(2)]
        ln1_stats = sem("ln1_stats")
        ln1_mv = sem("ln1_mv")
        ln1_var = sem("ln1_var")
        ln1_rstd = sem("ln1_rstd")
        xn_ready = sem("xn_ready")
        xnT_in_psum = sem("xnT_in_psum")
        xnT_ready = sem("xnT_ready")
        u_in_psum = sem("u_in_psum")
        u_ready = sem("u_ready")
        dtl_in_psum = sem("dtl_in_psum")
        dtl_ready = sem("dtl_ready")
        dt_raw = sem("dt_raw")
        dt_ready = sem("dt_ready")
        w_ready = sem("w_ready")
        bc_in_psum = sem("bc_in_psum")
        bc_ready = sem("bc_ready")
        z_in_psum = sem("z_in_psum")
        sz_ready = sem("sz_ready")
        wT_in_psum = sem("wT_in_psum")
        wT_ready = sem("wT_ready")
        dBT_ready = sem("dBT_ready")
        dB_in_psum = sem("dB_in_psum")
        exp_done = sem("exp_done")
        clamp_done = sem("clamp_done")
        scan_done = sem("scan_done")
        hT_in_psum = sem("hT_in_psum")
        mac_done = sem("mac_done")
        yb_in_psum = sem("yb_in_psum")
        yd_ready = sem("yd_ready")
        yz_ready = sem("yz_ready")
        op_in_psum = sem("op_in_psum")
        x1_ready = sem("x1_ready")
        ln2_stats = sem("ln2_stats")
        ln2_mv = sem("ln2_mv")
        ln2_var = sem("ln2_var")
        ln2_rstd = sem("ln2_rstd")
        xn2_ready = sem("xn2_ready")
        xn2T_in_psum = sem("xn2T_in_psum")
        xn2T_ready = sem("xn2T_ready")
        logit_in_psum = sem("logit_in_psum")
        logit_ready = sem("logit_ready")
        prob_ready = sem("prob_ready")
        route_step = sem("route_step")
        route_ready = sem("route_ready")
        gate_in_psum = sem("gate_in_psum")
        up_in_psum = sem("up_in_psum")
        silu_done = sem("silu_done")
        prod_done = sem("prod_done")
        down_in_psum = sem("down_in_psum")
        net_added = sem("net_added")
        out_stored = [sem(f"out_stored{j}") for j in range(2)]

        mixer_loads = [(win_sb, w_in), (wconv_sb, w_conv), (chan_sb, chan), (wz_sb, w_z),
                       (wdt_sb, w_dt), (wbc_sb, w_bc), (wout_sb, w_out), (wr_sb, w_router),
                       (br_sb, b_router)]
        expert_loads = [(wg_sb, w_gate), (wu_sb, w_up), (wd_sb, w_down)]
        MIXER_LOADED = 16 * len(mixer_loads)
        EXPERTS_LOADED = 16 * len(expert_loads)
        CONSTS = 4 + EXPERTS
        TAP_USES = TAPS // 2

        block = ctx.enter_context(nc.Block())

        @block.sync
        def _(sp):
            sp.dma_start(x_sb[:, 0], x_v[0]).then_inc(x_loaded[0], 16)
            for tile, src in mixer_loads:
                sp.dma_start(tile[:], src).then_inc(mixer_weights, 16)
            for tile, src in expert_loads:
                sp.dma_start(tile[:], src).then_inc(expert_weights, 16)

            def load_x(g, odd):
                at_least(sp, xn_ready, g - 1)
                sp.dma_start(x_sb[:, odd], x_v[bass.ds(g, 1)].rearrange("g p c d -> (g p) c d")
                             ).then_inc(x_loaded[odd], 16)

            def step(k, odd, scan, proj, tail):
                M = k - 1
                if scan and proj:
                    load_x(k + 1, 1 - odd)
                if scan:
                    at_least(sp, out_stored[odd], transfers(k, odd) - 16)
                    sp.dma_start(x1[:, odd], x_v[bass.ds(k, 1)].rearrange("g p c d -> (g p) c d")
                                 ).then_inc(res_loaded[odd], 16)
                if tail:
                    sp.wait_ge(net_added, NETS * (M + 1))
                    sp.dma_start(out_v[bass.ds(M, 1)].rearrange("g p c d -> (g p) c d"),
                                 x1[:, 1 - odd]).then_inc(out_stored[1 - odd], 16)

            run_steps(sp, step)
            for j in range(2):
                sp.wait_ge(out_stored[j], 16 * (GROUPS // 2))

        @block.gpsimd
        def _(pool):
            pool.memset(ident[:], 0.0).then_inc(ident_set, 1)
            pool.memset(xnT[:], 0.0).then_inc(consts, 1)
            pool.memset(dA[:], 0.0).then_inc(consts, 1)
            pool.memset(ones[:], 1.0).then_inc(consts, 1)
            pool.memset(neg_half[:], -0.5).then_inc(consts, 1)
            for e in range(EXPERTS):
                pool.memset(rank[:, e:e + 1], float(EXPERTS - e)).then_inc(consts, 1)
            pool.wait_ge(ident_set, 1)
            pool.affine_select(out=ident[:], in_=ident[:], compare_op=ALU.not_equal, fill=1.0,
                               base=0, pattern=[[-1, P]], channel_multiplier=1).then_inc(ident_set, 1)
            pool.wait_ge(consts, CONSTS)

            def rstd(g, mv, var_done, mv_done, done, rs):
                wait_apart(pool, mv_done, CHUNKS * (g + 1), pool_passed)
                pool.tensor_scalar(rs[:], mv[:, :, 1], LN_EPS, 1.0, ALU.add, ALU.mult).then_inc(var_done, 1)
                pool.wait_ge(var_done, g + 1)
                pool.tensor_tensor(rs[:], rs[:], neg_half[:], ALU.pow).then_inc(done, 1)

            def state_input(g, n, odd):
                j = NS * g + n
                for half in range(HALVES):
                    wait_apart(pool, exp_done, 2 * j + half + 1, pool_passed)
                    part = dA[:, n % DA_RING, half].rearrange("p (s t) -> p s t", s=SPG)[:, :, 1:]
                    pool.tensor_scalar(part, part, float(np.exp(np.float32(CLIP))),
                                       float(np.exp(np.float32(-CLIP))),
                                       ALU.min, ALU.max).then_inc(clamp_done, 1)
                if n == 0:
                    pool.wait_ge(wT_ready, 2 * (g + 1))
                    pool.wait_ge(bc_ready, g + 1)
                wait_apart(pool, dB_in_psum, 2 * (j - DB_RING + 1), pool_passed)
                for c in range(CHUNKS):
                    op = pool.tensor_scalar(dBT[:, n % DB_RING, c], wT[:, odd, c],
                                            bc[:, odd, c, n:n + 1], STATE_EPS, ALU.mult, ALU.add)
                op.then_inc(dBT_ready, 1)

            def step(k, odd, scan, proj, tail):
                G, M = k + 1, k - 1
                for s in range(SLOTS):
                    n = s + LEAD
                    if n < NS and scan:
                        state_input(k, n, odd)
                    if n >= NS and proj:
                        state_input(G, n - NS, 1 - odd)
                    if s == 0 and proj:
                        rstd(G, mv1, ln1_var, ln1_mv, ln1_rstd, rstd1)
                    if s in (1, 2) and tail:
                        half = s - 1
                        pool.wait_ge(yd_ready, 2 * M + half + 1)
                        at_least(pool, op_in_psum, M)
                        pool.tensor_tensor(yz[:, half], yd[:, half], sz[:, 1 - odd, half],
                                           ALU.mult).then_inc(yz_ready, 1)
                    if s == 3 and tail:
                        rstd(M, mv2, ln2_var, ln2_mv, ln2_rstd, rstd2)
                    if s == 7 and proj:
                        pool.wait_ge(dt_ready, G + 1)
                        at_least(pool, wT_in_psum, 2 * G)
                        pool.tensor_tensor(w_sb[:], dt_sb[:, 1 - odd], u_sb[:, 1 - odd],
                                           ALU.mult).then_inc(w_ready, 1)

            run_steps(pool, step)

        @block.scalar
        def _(act):
            act.wait_ge(mixer_weights, MIXER_LOADED)
            act.activation(A_sb[:], chan_sb[:, :, 0:NS], ACT.Exp).then_inc(a_exp, 1)
            act.wait_ge(a_exp, 1)
            act.activation(A_sb[:], A_sb[:], ACT.Copy, scale=-1.0).then_inc(a_ready, 1)
            for j in range(TAP_USES):
                act.wait_ge(tap_in_psum, j + 1)
                act.activation(wtap[:, 2 * j:2 * j + 2], p_misc[:].rearrange("p (k c) -> p k c", k=2),
                               ACT.Copy).then_inc(tap_ready, 1)
            act.wait_ge(a_ready, 1)
            act.wait_ge(consts, CONSTS)

            def decays(g, n0, odd):
                if n0 == 0:
                    act.wait_ge(dt_ready, g + 1)
                for n in range(n0, n0 + 4):
                    j = NS * g + n
                    at_least(act, scan_done, 2 * (j - DA_RING + 1))
                    for half in range(HALVES):
                        src = dt_sb[:, odd, half].rearrange("p (s t) -> p s t", s=SPG)
                        dst = dA[:, n % DA_RING, half].rearrange("p (s t) -> p s t", s=SPG)
                        act.activation(dst[:, :, 1:], src[:, :, 1:], ACT.Exp,
                                       scale=A_sb[:, half, n:n + 1]).then_inc(exp_done, 1)

            def step(k, odd, scan, proj, tail):
                G, M = k + 1, k - 1
                for s in range(SLOTS):
                    if s in EXP_SLOTS:
                        n0 = EXP_SLOTS[s]
                        if n0 and scan:
                            decays(k, n0, odd)
                        if n0 == 0 and proj:
                            decays(G, 0, 1 - odd)
                    if s == 6 and proj:
                        act.wait_ge(dtl_ready, 2 * (G + 1))
                        act.activation(dt_sb[:, 1 - odd], dtl[:], ACT.Sigmoid).then_inc(dt_raw, 1)
                    if s == 6 and tail:
                        act.wait_ge(logit_ready, M + 1)
                        at_least(act, route_ready, M)
                        act.activation(prob[:], logit[:], ACT.Sigmoid).then_inc(prob_ready, 1)
                    if s == 1 and proj:
                        act.wait_ge(xnT_in_psum, G + 1)
                        at_least(act, z_in_psum, 2 * G)
                        act.activation(xnT[:, :, TAPS - 1:], p_misc[:].rearrange("p (s t) -> p s t", s=SPG),
                                       ACT.Copy).then_inc(xnT_ready, 1)
                    if s in (2, 3) and proj:
                        half = s - 2
                        act.wait_ge(u_in_psum, 2 * G + half + 1)
                        if tail:
                            act.wait_ge(yd_ready, 2 * M + half + 1)
                        act.activation(u_sb[:, 1 - odd, half], p_misc[:], ACT.Identity,
                                       bias=chan_sb[:, half, NS:NS + 1]).then_inc(u_ready, 1)
                    if s in (4, 5) and proj:
                        half = s - 4
                        act.wait_ge(dtl_in_psum, 2 * G + half + 1)
                        act.activation(dtl[:, half], p_misc[:], ACT.Identity,
                                       bias=chan_sb[:, half, NS + 1:NS + 2]).then_inc(dtl_ready, 1)
                    if s == 4 and tail:
                        act.wait_ge(xn2T_in_psum, M + 1)
                        at_least(act, up_in_psum, UNITS * M)
                        act.activation(xn2T[:], p_misc[:], ACT.Copy).then_inc(xn2T_ready, 1)
                    if s == 5 and tail:
                        act.wait_ge(logit_in_psum, M + 1)
                        act.activation(logit[:], p_misc[:, 0:CHUNKS * EXPERTS].rearrange(
                            "p (c e) -> p c e", c=CHUNKS), ACT.Copy).then_inc(logit_ready, 1)
                    if s == 6 and proj:
                        act.wait_ge(bc_in_psum, G + 1)
                        if tail:
                            act.wait_ge(mac_done, PAIRS * NS * k)
                        act.activation(bc[:, 1 - odd], p_misc[:, 0:CHUNKS * 2 * NS].rearrange(
                            "p (c n) -> p c n", c=CHUNKS), ACT.Copy).then_inc(bc_ready, 1)
                    if s in (6, 7) and proj:
                        half = s - 6
                        act.wait_ge(z_in_psum, 2 * G + half + 1)
                        if tail:
                            act.wait_ge(yz_ready, 2 * (M + 1))
                        act.activation(sz[:, 1 - odd, half], p_misc[:], ACT.Silu).then_inc(sz_ready, 1)
                    if s in (8, 9) and proj:
                        pair = s - 8
                        act.wait_ge(wT_in_psum, 2 * G + pair + 1)
                        at_least(act, dBT_ready, NS * k)
                        act.activation(wT[:, 1 - odd, 2 * pair:2 * pair + 2],
                                       p_misc[:].rearrange("p (c w) -> p c w", c=2),
                                       ACT.Copy).then_inc(wT_ready, 1)
                    for i in UNITS_OF_SLOT[s] if tail else []:
                        act.wait_ge(gate_in_psum, UNITS * M + i + 1)
                        at_least(act, prod_done, UNITS * M + max(i - 1, 0))
                        act.activation(sg[:, i % 2], p_gate[:], ACT.Silu).then_inc(silu_done, 1)

            run_steps(act, step)

        @block.tensor
        def _(pe):
            pe.wait_ge(mixer_weights, MIXER_LOADED)
            pe.wait_ge(ident_set, 2)
            pe.wait_ge(consts, CONSTS)
            for j in range(TAP_USES):
                at_least(pe, tap_ready, j)
                for q in range(2):
                    for half in range(HALVES):
                        mm = pe.matmul(p_misc[:, q * CH:(q + 1) * CH], win_sb[:, half],
                                       wconv_sb[:, half, 2 * j + q],
                                       start=half == 0, stop=half == HALVES - 1)
                mm.then_inc(tap_in_psum, 1)
            pe.wait_ge(tap_ready, TAP_USES)

            def inputs_by_channel(g, n, half):
                j = NS * g + n
                pe.wait_ge(dBT_ready, j + 1)
                at_least(pe, scan_done, 2 * (j - 1) + half + 1)
                for c in range(CHUNKS):
                    mm = pe.transpose(p_dB[half][:, c * P:(c + 1) * P],
                                      dBT[:, n % DB_RING, c, half * P:(half + 1) * P], ident[:])
                mm.then_inc(dB_in_psum, 1)

            def states_by_token(g, n):
                j = NS * g + n
                pe.wait_ge(scan_done, 2 * j + 2)
                for pair in range(PAIRS):
                    at_least(pe, mac_done, PAIRS * (j - 1) + pair + 1)
                    for c in range(2):
                        for half in range(HALVES):
                            t0 = (2 * pair + c) * P
                            mm = pe.transpose(p_hT[pair][:, c, half * P:(half + 1) * P],
                                              h[:, n % 2, half, t0:t0 + P], ident[:])
                    mm.then_inc(hT_in_psum, 1)

            def use_xnT(G):
                pe.wait_ge(xn_ready, G + 1)
                at_least(pe, wT_ready, 2 * G)
                for c in range(CHUNKS):
                    mm = pe.transpose(p_misc[:, c * P:(c + 1) * P], xn[:, c], ident[:])
                mm.then_inc(xnT_in_psum, 1)

            def use_yback(M, half, odd, proj):
                pe.wait_ge(mac_done, PAIRS * NS * (M + 1))
                if half == 0:
                    if proj:
                        pe.wait_ge(xnT_ready, M + 3)
                    else:
                        pe.wait_ge(wT_ready, 2 * GROUPS)
                        at_least(pe, logit_ready, M)
                else:
                    if proj:
                        pe.wait_ge(u_ready, 2 * (M + 2) + 1)
                    pe.wait_ge(yd_ready, 2 * M + 1)
                for c in range(CHUNKS):
                    mm = pe.transpose(p_misc[:, c * P:(c + 1) * P],
                                      yT[:, odd, c, half * P:(half + 1) * P], ident[:])
                mm.then_inc(yb_in_psum, 1)

            def use_u(G, half, tail):
                if half == 0:
                    pe.wait_ge(xnT_ready, G + 1)
                else:
                    pe.wait_ge(u_ready, 2 * G + 1)
                if tail:
                    pe.wait_ge(yd_ready, 2 * (G - 2) + half + 1)
                for t in range(TAPS):
                    mm = pe.matmul(p_misc[:].rearrange("p (s t) -> p s t", s=SPG),
                                   wtap[:, t, half * P:(half + 1) * P], xnT[:, :, t:t + SEQ],
                                   start=t == 0, stop=t == TAPS - 1)
                mm.then_inc(u_in_psum, 1)

            def use_outproj(M, proj):
                pe.wait_ge(yz_ready, 2 * (M + 1))
                if proj:
                    pe.wait_ge(u_ready, 2 * (M + 3))
                for c in range(CHUNKS):
                    for half in range(HALVES):
                        mm = pe.matmul(p_misc[:, c * DM:(c + 1) * DM], yz[:, half, c * P:(c + 1) * P],
                                       wout_sb[:, half], start=half == 0, stop=half == HALVES - 1)
                mm.then_inc(op_in_psum, 1)

            def use_dt(G, half, tail, odd):
                pe.wait_ge(u_ready, 2 * (G + 1))
                if tail:
                    if half == 0:
                        pe.wait_ge(x1_ready, G - 1)
                    else:
                        pe.wait_ge(xn2T_ready, G - 1)
                if half == 1:
                    pe.wait_ge(dtl_ready, 2 * G + 1)
                for q in range(HALVES):
                    mm = pe.matmul(p_misc[:], wdt_sb[:, q, half * P:(half + 1) * P],
                                   u_sb[:, odd, q], start=q == 0, stop=q == HALVES - 1)
                mm.then_inc(dtl_in_psum, 1)

            def use_xn2T(M, proj):
                pe.wait_ge(xn2_ready, M + 1)
                if proj:
                    pe.wait_ge(dtl_ready, 2 * (M + 2) + 1)
                for c in range(CHUNKS):
                    mm = pe.transpose(p_misc[:, c * P:(c + 1) * P], xn2[:, c], ident[:])
                mm.then_inc(xn2T_in_psum, 1)

            def use_logit(M, proj):
                pe.wait_ge(xn2T_ready, M + 1)
                if proj:
                    pe.wait_ge(dtl_ready, 2 * (M + 3))
                for c in range(CHUNKS):
                    o = p_misc[:, c * EXPERTS:(c + 1) * EXPERTS]
                    pe.matmul(o, xn2T[:, c * P:(c + 1) * P], wr_sb[:], start=True, stop=False)
                    mm = pe.matmul(o, ones[:], br_sb[:], start=False, stop=True)
                mm.then_inc(logit_in_psum, 1)

            def use_bc(G, tail, odd):
                if tail:
                    pe.wait_ge(logit_ready, G - 1)
                pe.wait_ge(dtl_ready, 2 * (G + 1))
                for c in range(CHUNKS):
                    for q in range(HALVES):
                        mm = pe.matmul(p_misc[:, c * 2 * NS:(c + 1) * 2 * NS],
                                       u_sb[:, odd, q, c * P:(c + 1) * P], wbc_sb[:, q],
                                       start=q == 0, stop=q == HALVES - 1)
                mm.then_inc(bc_in_psum, 1)

            def use_z(G, half):
                if half == 0:
                    pe.wait_ge(bc_ready, G + 1)
                else:
                    pe.wait_ge(sz_ready, 2 * G + 1)
                pe.matmul(p_misc[:].rearrange("p (s t) -> p s t", s=SPG),
                          wz_sb[:, half * P:(half + 1) * P], xnT[:, :, TAPS - 1:],
                          start=True, stop=True).then_inc(z_in_psum, 1)

            def use_wT(G, pair):
                if pair == 0:
                    pe.wait_ge(sz_ready, 2 * (G + 1))
                    pe.wait_ge(w_ready, G + 1)
                else:
                    pe.wait_ge(wT_ready, 2 * G + 1)
                for c in range(2):
                    for half in range(HALVES):
                        t0 = (2 * pair + c) * P
                        mm = pe.transpose(p_misc[:, c * CH + half * P:c * CH + (half + 1) * P],
                                          w_sb[:, half, t0:t0 + P], ident[:])
                mm.then_inc(wT_in_psum, 1)

            def gate_up(M, i):
                e, half = divmod(i, 2)
                if i == 0:
                    pe.wait_ge(xn2T_ready, M + 1)
                at_least(pe, prod_done, UNITS * M + i)
                pe.matmul(p_gate[:], wg_sb[:, e, half * P:(half + 1) * P], xn2T[:],
                          start=True, stop=True).then_inc(gate_in_psum, 1)
                pe.matmul(p_up[:], wu_sb[:, e, half * P:(half + 1) * P], xn2T[:],
                          start=True, stop=True).then_inc(up_in_psum, 1)

            def down(M, e):
                pe.wait_ge(prod_done, UNITS * M + 2 * e + 2)
                at_least(pe, net_added, NETS * M + e)
                for c in range(CHUNKS):
                    for half in range(2):
                        mm = pe.matmul(p_down[:, c], hm[:, e % 2, half, c * P:(c + 1) * P],
                                       wd_sb[:, e, half], start=half == 0, stop=half == 1)
                mm.then_inc(down_in_psum, 1)

            def step(k, odd, scan, proj, tail):
                G, M = k + 1, k - 1
                for s in range(SLOTS):
                    if s + 1 < NS and scan:
                        inputs_by_channel(k, s + 1, 0)
                    if s + 1 == NS and proj:
                        inputs_by_channel(G, 0, 0)
                    if s == 1 and proj:
                        use_xnT(G)
                    if s == 1 and tail:
                        use_yback(M, 0, 1 - odd, proj)
                    if s == 2 and proj:
                        use_u(G, 0, tail)
                    if s == 2 and tail:
                        use_yback(M, 1, 1 - odd, proj)
                    if s == 3 and proj:
                        use_u(G, 1, tail)
                    if s == 3 and tail:
                        use_outproj(M, proj)
                    if s == 4 and proj:
                        use_dt(G, 0, tail, 1 - odd)
                    if s == 4 and tail:
                        use_xn2T(M, proj)
                    if s == 5 and proj:
                        use_dt(G, 1, tail, 1 - odd)
                    if s == 5 and tail:
                        use_logit(M, proj)
                    if s == 6 and proj:
                        use_bc(G, tail, 1 - odd)
                    if s in (6, 7) and proj:
                        use_z(G, s - 6)
                    if s in (8, 9) and proj:
                        use_wT(G, s - 8)
                    for i in UNITS_OF_SLOT[s] if tail else []:
                        gate_up(M, i)
                        if i >= 2 and i % 2 == 0:
                            down(M, i // 2 - 1)
                        if i == UNITS - 1:
                            down(M, NETS - 1)
                    if s + 1 < NS and scan:
                        inputs_by_channel(k, s + 1, 1)
                    if s + 1 == NS and proj:
                        inputs_by_channel(G, 0, 1)
                    if scan:
                        states_by_token(k, s)

            pe.wait_ge(expert_weights, EXPERTS_LOADED)
            run_steps(pe, step)

        @block.vector
        def _(dve):
            dve.wait_ge(consts, CONSTS)

            def scan_state(g, n):
                j = NS * g + n
                at_least(dve, hT_in_psum, PAIRS * (j - 1))
                for half in range(HALVES):
                    dve.wait_ge(dB_in_psum, 2 * j + half + 1)
                    dve.wait_ge(clamp_done, 2 * j + half + 1)
                    dve.tensor_tensor_scan(h[:, n % 2, half], dA[:, n % DA_RING, half],
                                           p_dB[half][:], 0.0, ALU.mult, ALU.add).then_inc(scan_done, 1)

            def sum_states(g, n, odd):
                j = NS * g + n
                for pair in range(PAIRS):
                    dve.wait_ge(hT_in_psum, PAIRS * j + pair + 1)
                    if n == 0 and pair == 0:
                        dve.wait_ge(bc_ready, g + 1)
                        at_least(dve, yb_in_psum, 2 * (g - 1))
                    at_least(dve, mac_done, PAIRS * (j - 1) + pair + 1)
                    for c in range(2):
                        cc = 2 * pair + c
                        scalar = bc[:, odd, cc, NS + n:NS + n + 1]
                        if n == 0:
                            op = dve.tensor_scalar(yT[:, odd, cc], p_hT[pair][:, c], scalar, None, ALU.mult)
                        else:
                            op = dve.scalar_tensor_tensor(yT[:, odd, cc], p_hT[pair][:, c], scalar,
                                                          yT[:, odd, cc], ALU.mult, ALU.add)
                    op.then_inc(mac_done, 1)

            def norm_stats(g, src, stats, mv, stats_done, mv_done):
                for c in range(CHUNKS):
                    dve.bn_stats(stats[:, c], src[:, c]).then_inc(stats_done, 1)
                wait_apart(dve, stats_done, CHUNKS * (g + 1), dve_passed)
                for c in range(CHUNKS):
                    dve.bn_aggr(mv[:, c], stats[:, c]).then_inc(mv_done, 1)

            def norm_apply(dst, src, mv, rs, done):
                for c in range(CHUNKS):
                    op = dve.tensor_scalar(dst[:, c], src[:, c], mv[:, c, 0:1], rs[:, c:c + 1],
                                           ALU.subtract, ALU.mult)
                op.then_inc(done, 1)

            def pick_experts(M):
                dve.wait_ge(prob_ready, M + 1)
                wide = [P, CHUNKS, EXPERTS]
                rank_b = rank[:].rearrange("p (o e) -> p o e", o=1).broadcast_to(wide)

                def spread(v):
                    return v[:].rearrange("p (c o) -> p c o", o=1).broadcast_to(wide)

                count = [0]

                def then(op):
                    count[0] += 1
                    op.then_inc(route_step, 1)
                    dve.wait_ge(route_step, ROUTE_STEPS * M + count[0])

                src = prob
                for j in range(2):
                    then(dve.tensor_reduce(top[j][:], src[:], AX.X, ALU.max))
                    then(dve.tensor_tensor(key[:], src[:], spread(top[j]), ALU.is_equal))
                    then(dve.tensor_tensor(key[:], key[:], rank_b, ALU.mult))
                    then(dve.tensor_reduce(win[:], key[:], AX.X, ALU.max))
                    then(dve.tensor_tensor(hit[j][:], key[:], spread(win), ALU.is_equal))
                    if j == 0:
                        then(dve.scalar_tensor_tensor(rest[:], hit[0][:], -2.0, prob[:], ALU.mult, ALU.add))
                        src = rest
                then(dve.tensor_tensor(win[:], top[0][:], top[1][:], ALU.add))
                then(dve.reciprocal(share[:], win[:]))
                then(dve.tensor_tensor(key[:], hit[0][:], hit[1][:], ALU.add))
                op = dve.tensor_tensor(key[:], key[:], spread(share), ALU.mult)
                then(op)
                assert count[0] == ROUTE_STEPS
                dve.tensor_tensor(route[:], key[:], prob[:], ALU.mult).then_inc(route_ready, 1)

            def product(M, i):
                e, half = divmod(i, 2)
                dve.wait_ge(silu_done, UNITS * M + i + 1)
                dve.wait_ge(up_in_psum, UNITS * M + i + 1)
                at_least(dve, down_in_psum, NETS * M + max(e - 1, 0))
                dve.tensor_tensor(hm[:, e % 2, half], p_up[:], sg[:, i % 2], ALU.mult).then_inc(prod_done, 1)

            def add_net(M, e, odd):
                dve.wait_ge(down_in_psum, NETS * M + e + 1)
                at_least(dve, net_added, NETS * M + e)
                if e == 0:
                    dve.tensor_tensor(x1[:, odd], p_down[:], x1[:, odd], ALU.add).then_inc(net_added, 1)
                    return
                if e == 1:
                    dve.wait_ge(route_ready, M + 1)
                for c in range(CHUNKS):
                    op = dve.scalar_tensor_tensor(x1[:, odd, c], p_down[:, c], route[:, c, e - 1:e],
                                                  x1[:, odd, c], ALU.mult, ALU.add)
                op.then_inc(net_added, 1)

            def step(k, odd, scan, proj, tail):
                G, M = k + 1, k - 1
                for s in range(SLOTS):
                    if scan:
                        scan_state(k, s)
                    if s > 0 and scan:
                        sum_states(k, s - 1, odd)
                    if s == 0 and tail:
                        sum_states(M, NS - 1, 1 - odd)
                    if s == 0 and proj:
                        dve.wait_ge(x_loaded[1 - odd], transfers(G, 1 - odd))
                        at_least(dve, ln1_rstd, G)
                        norm_stats(G, x_sb[:, 1 - odd], stats1, mv1, ln1_stats, ln1_mv)
                    if s == 1 and proj:
                        dve.wait_ge(ln1_rstd, G + 1)
                        at_least(dve, xnT_in_psum, G)
                        norm_apply(xn, x_sb[:, 1 - odd], mv1, rstd1, xn_ready)
                    if s in (1, 2) and tail:
                        half = s - 1
                        dve.wait_ge(yb_in_psum, 2 * M + half + 1)
                        at_least(dve, yz_ready, 2 * M)
                        dve.scalar_tensor_tensor(yd[:, half], u_sb[:, 1 - odd, half],
                                                 chan_sb[:, half, NS + 2:NS + 3], p_misc[:],
                                                 ALU.mult, ALU.add).then_inc(yd_ready, 1)
                    if s == 3 and tail:
                        dve.wait_ge(op_in_psum, M + 1)
                        dve.wait_ge(res_loaded[1 - odd], transfers(M, 1 - odd))
                        dve.tensor_tensor(x1[:, 1 - odd], p_misc[:].rearrange("p (c d) -> p c d", c=CHUNKS),
                                          x1[:, 1 - odd], ALU.add).then_inc(x1_ready, 1)
                        dve.wait_ge(x1_ready, M + 1)
                        at_least(dve, ln2_rstd, M)
                        norm_stats(M, x1[:, 1 - odd], stats2, mv2, ln2_stats, ln2_mv)
                    if s == 4 and tail:
                        dve.wait_ge(ln2_rstd, M + 1)
                        at_least(dve, xn2T_in_psum, M)
                        norm_apply(xn2, x1[:, 1 - odd], mv2, rstd2, xn2_ready)
                    if s == 6 and proj:
                        dve.wait_ge(dt_raw, G + 1)
                        dve.tensor_scalar(dt_sb[:, 1 - odd], dt_sb[:, 1 - odd], DT_MIN, 1.0,
                                          ALU.max, ALU.min).then_inc(dt_ready, 1)
                    for i in UNITS_OF_SLOT[s] if tail else []:
                        product(M, i)
                        if i >= 3 and i % 2 == 1:
                            add_net(M, (i - 3) // 2, 1 - odd)
                        if i == UNITS - 1:
                            add_net(M, NETS - 1, 1 - odd)
                    if s == 7 and tail:
                        pick_experts(M)

            run_steps(dve, step)


_OUT = "out_dram"


def kernel(**inputs):
    import concourse.bacc as bacc
    from concourse.bass_utils import run_bass_kernel_spmd

    a = {n: np.asarray(v) for n, v in inputs.items()}
    x = a["L0_attn_x"]

    def parts(m):
        return m.reshape((m.shape[0] // P, P) + m.shape[1:]).swapaxes(0, 1)

    w_in = a["L0_attn_in_proj_w"]
    gates = np.concatenate([a["L0_ffn_sg_w"][None], a["L0_ffn_wg"]])
    ups = np.concatenate([a["L0_ffn_su_w"][None], a["L0_ffn_wu"]])
    downs = np.concatenate([a["L0_ffn_sd_w"][None], a["L0_ffn_wd"]])
    arrays = {
        "x": x.reshape(TOKENS, DM),
        "w_in": parts(w_in[:CH]),
        "w_z": w_in[CH:].T,
        "w_conv": parts(a["L0_attn_conv_w"].transpose(1, 2, 0)),
        "w_dt": parts(a["L0_attn_dt_w"].T),
        "w_bc": parts(np.concatenate([a["L0_attn_B_w"], a["L0_attn_C_w"]]).T),
        "w_out": parts(a["L0_attn_out_w"].T),
        "chan": parts(np.concatenate([a["L0_attn_A_log"], a["L0_attn_conv_b"][:, None],
                                      a["L0_attn_dt_b"][:, None], a["L0_attn_D"][:, None]], axis=1)),
        "w_router": a["L0_ffn_router_w"].T,
        "b_router": a["L0_ffn_routing_bias"][None],
        "w_gate": gates.transpose(2, 0, 1),
        "w_up": ups.transpose(2, 0, 1),
        "w_down": downs.transpose(2, 0, 1).reshape(2, P, NETS, DM).transpose(1, 2, 0, 3),
    }
    nc = bacc.Bacc("TRN2", target_bir_lowering=False, num_devices=1)
    feed, args = {}, []
    for name, arr in arrays.items():
        arr = np.ascontiguousarray(arr)
        feed[f"{name}_dram"] = arr
        args.append(nc.dram_tensor(f"{name}_dram", arr.shape, mybir.dt.from_np(arr.dtype),
                                   kind="ExternalInput").ap())
    out = nc.dram_tensor(_OUT, (TOKENS, DM), F32, kind="ExternalOutput").ap()
    build(nc, *args, out)
    r = run_bass_kernel_spmd(nc, [feed], core_ids=[0])
    return r.results[0][_OUT].reshape(x.shape)
```

```python
from contextlib import ExitStack

import numpy as np
import concourse.bass as bass
from concourse import mybir

F32 = mybir.dt.float32
F32R = mybir.dt.float32r
ALU = mybir.AluOpType
ACT = mybir.ActivationFunctionType
AX = mybir.AxisListType

P = 128
DM = 128
CH = 256
HALVES = CH // P
NS = 16
TAPS = 4
SEQ = 256
TOKENS = 32 * SEQ
TOK = 512
SPG = TOK // SEQ
CHUNKS = TOK // P
PAIRS = CHUNKS // 2
GROUPS = TOKENS // TOK
SLOTS = NS
EXPERTS = 8
NETS = EXPERTS + 1
HID = 256
UNITS = 2 * NETS
LN_EPS = 1e-5
STATE_EPS = 1e-6
CLIP = 5.0
DT_MIN = 1e-4
DA_RING = 8
DB_RING = 4
EXP_SLOTS = {2: (4, 5), 3: (6, 7), 6: (8, 9), 7: (10, 11), 10: (12, 13), 11: (14, 15),
             14: (0, 1), 15: (2, 3)}
CLAMP_LEAD, EPS_LEAD, INPUT_LEAD, ROW_LEAD = 1, 2, 3, 5
ROUTE_STEPS = 15
ALL = slice(None)


GU, DN = "gate_up", "down"
WORK = {0: [(GU, 0), (GU, 1)], 1: [(GU, 2), (DN, 0), (GU, 3)], 2: [(DN, 1)], 3: [],
        4: [(GU, 4), (GU, 5)], 5: [(GU, 6), (DN, 2), (GU, 7), (GU, 8)], 6: [(DN, 3)], 7: [],
        8: [(GU, 9), (GU, 10)], 9: [(GU, 11), (DN, 4), (GU, 12)], 10: [(DN, 5)], 11: [],
        12: [(GU, 13), (GU, 14)], 13: [(GU, 15), (DN, 6), (GU, 16), (GU, 17)], 14: [(DN, 7)],
        15: [(DN, 8)]}


def at_least(eng, sem, value):
    if isinstance(value, int) and value <= 0:
        return
    eng.wait_ge(sem, value)


def wait_apart(eng, sem, value, passed):
    if isinstance(value, int) and value <= 0:
        return
    eng.wait_ge(sem, value)
    if not isinstance(value, int):
        eng.sem_inc(passed, 1)


def transfers(g, odd):
    return 8 * (g - odd) + 16


def run_steps(eng, step):
    step(-1, 1, False, True, False, False)
    step(0, 0, True, True, False, False)
    step(1, 1, True, True, True, False)
    step(2, 0, True, True, True, True)
    with eng.Fori(0, GROUPS // 2 - 2) as pair:
        step(2 * pair + 3, 1, True, True, True, True)
        step(2 * pair + 4, 0, True, True, True, True)
    step(GROUPS - 1, 1, True, False, True, True)
    step(GROUPS, 0, False, False, True, True)
    step(GROUPS + 1, 1, False, False, False, True)


def build(nc, x, w_in, w_z, w_conv, w_dt, w_bc, w_out, chan, w_router, b_router,
          w_gate, w_up, w_down, b_rows, out):
    x_v = x.rearrange("(g c p) d -> g p c d", c=CHUNKS, p=P)
    out_v = out.rearrange("(g c p) d -> g p c d", c=CHUNKS, p=P)

    ctx = ExitStack()
    with ctx:
        def sb(name, shape, dtype=F32):
            return ctx.enter_context(nc.sbuf_tensor(name, shape, dtype))

        def sb_split(name, shape):
            return sb(f"{name}_hi", shape, F32R), sb(f"{name}_lo", shape, F32R)

        def pb(name, shape):
            return ctx.enter_context(nc.psum_tensor(name, shape, F32))

        def sem(name):
            return ctx.enter_context(nc.semaphore(name))

        ident = sb("ident", [P, P])
        wz_s = sb_split("wz_s", [P, CH])
        wtap_s = sb_split("wtap_s", [P, TAPS, CH])
        wdt_s = sb_split("wdt_s", [P, HALVES, CH])
        wbc_sb = sb("wbc_sb", [P, HALVES, 2 * NS])
        wout_sb = sb("wout_sb", [P, HALVES, DM])
        chan_sb = sb("chan_sb", [P, HALVES, NS + 3])
        A_sb = sb("A_sb", [P, HALVES, NS])
        wbc_s = sb_split("wbc_s", [P, HALVES, 2 * NS])
        wr_sb = sb("wr_sb", [P, EXPERTS])
        wr_s = sb_split("wr_s", [P, EXPERTS])
        br_sb = sb("br_sb", [1, EXPERTS])
        ones = sb("ones", [1, P])
        rank = sb("rank", [P, EXPERTS])
        neg_half = sb("neg_half", [P, CHUNKS])
        wg_s = sb_split("wg_s", [P, NETS, HID])
        wu_s = sb_split("wu_s", [P, NETS, HID])
        wd_sb = sb("wd_sb", [P, NETS, 2, DM])

        amin = sb("amin", [P, 1])
        amin_all = sb("amin_all", [1, 1])
        flag = ctx.enter_context(nc.sbuf_tensor("flag", [1, 1], mybir.dt.int32))

        x_sb = sb("x_sb", [P, 2, CHUNKS, DM])
        stats1 = sb("stats1", [P, CHUNKS, 6])
        mv1 = sb("mv1", [P, CHUNKS, 2])
        rstd1 = sb("rstd1", [P, CHUNKS])
        xn = sb("xn", [P, CHUNKS, DM])
        xnT_s = sb_split("xnT_s", [P, SPG, TAPS - 1 + SEQ])
        u_sb = sb("u_sb", [P, 2, HALVES, TOK])
        u_s = sb_split("u_s", [P, HALVES, TOK])
        turns = sb("turns", [P, HALVES, TOK])
        yz = dtl = turns
        dt_sb = sb("dt_sb", [P, HALVES, TOK])
        w_sb = sb("w_sb", [P, HALVES, TOK])
        c_sb = sb("c_sb", [P, 2, CHUNKS, NS])
        brow = sb("brow", [P, DB_RING, TOK])
        sz = sb("sz", [P, 2, HALVES, TOK])
        dA = sb("dA", [P, DA_RING, HALVES, TOK])
        stage = dA[:].rearrange("p n h t -> p (n h t)")
        wg_sb = stage[:, 0:NETS * HID].rearrange("p (e i) -> p e i", e=NETS)
        wu_sb = stage[:, NETS * HID:2 * NETS * HID].rearrange("p (e i) -> p e i", e=NETS)
        wconv_sb = stage[:, 2 * NETS * HID:2 * NETS * HID + HALVES * TAPS * CH].rearrange(
            "p (h k c) -> p h k c", h=HALVES, k=TAPS)
        dB = sb("dB", [P, DB_RING, HALVES, TOK])
        stage_b = dB[:].rearrange("p n h t -> p (n h t)")

        def staged(at, n):
            return stage_b[:, at:at + n]

        wtap = staged(0, TAPS * CH).rearrange("p (k c) -> p k c", k=TAPS)
        wz_sb = staged(TAPS * CH, CH)
        wdt_sb = staged((TAPS + 1) * CH, HALVES * CH).rearrange("p (h c) -> p h c", h=HALVES)
        win_sb = staged((TAPS + 3) * CH, HALVES * DM).rearrange("p (h d) -> p h d", h=HALVES)
        h = sb("h", [P, 2, HALVES, TOK])
        yT = sb("yT", [P, 2, CHUNKS, CH])
        res = sb("res", [P, CHUNKS, DM])
        x1 = sb("x1", [P, 2, CHUNKS, DM])
        stats2 = sb("stats2", [P, CHUNKS, 6])
        mv2 = sb("mv2", [P, CHUNKS, 2])
        rstd2 = sb("rstd2", [P, CHUNKS])
        xn2 = xn
        b_sb = xn[0:NS].rearrange("p c d -> p (c d)")
        xn2T_s = [sb_split(f"xn2T_s{j}", [P, TOK]) for j in range(2)]
        logit = sb("logit", [P, CHUNKS, EXPERTS])
        prob = sb("prob", [P, CHUNKS, EXPERTS])
        hit = [sb(f"hit{j}", [P, CHUNKS, EXPERTS]) for j in range(2)]
        key = sb("key", [P, CHUNKS, EXPERTS])
        rest = sb("rest", [P, CHUNKS, EXPERTS])
        top = [sb(f"top{j}", [P, CHUNKS]) for j in range(2)]
        win = sb("win", [P, CHUNKS])
        share = sb("share", [P, CHUNKS])
        route = sb("route", [P, 2, CHUNKS, EXPERTS])
        hm = sb("hm", [P, 2, 2, TOK])

        p_hT = [pb(f"p_hT{i}", [P, 2, CH]) for i in range(PAIRS)]
        p_gate = [pb(f"p_gate{i}", [P, TOK]) for i in range(2)]
        p_up = [pb(f"p_up{i}", [P, TOK]) for i in range(2)]
        p_down = pb("p_down", [P, CHUNKS, DM])
        p_misc = pb("p_misc", [P, TOK])

        mixer_weights = sem("mixer_weights")
        expert_weights = sem("expert_weights")
        consts = sem("consts")
        pool_passed = sem("pool_passed")
        sp_passed = sem("sp_passed")
        dve_passed = sem("dve_passed")
        ident_set = sem("ident_set")
        a_exp = sem("a_exp")
        a_ready = sem("a_ready")
        amin_ready = sem("amin_ready")
        amin_in_psum = sem("amin_in_psum")
        flag_ready = sem("flag_ready")
        tap_in_psum = sem("tap_in_psum")
        tap_ready = sem("tap_ready")
        mixer_hi = sem("mixer_hi")
        mixer_split = sem("mixer_split")
        starts_zeroed = sem("starts_zeroed")
        expert_hi = sem("expert_hi")
        expert_split = sem("expert_split")
        x_loaded = [sem(f"x_loaded{j}") for j in range(2)]
        res_loaded = sem("res_loaded")
        ln1_stats = sem("ln1_stats")
        ln1_mv = sem("ln1_mv")
        ln1_var = sem("ln1_var")
        ln1_rstd = sem("ln1_rstd")
        xn_ready = sem("xn_ready")
        xnT_in_psum = sem("xnT_in_psum")
        xnT_hi_ready = sem("xnT_hi_ready")
        xnT_ready = sem("xnT_ready")
        u_in_psum = sem("u_in_psum")
        u_ready = sem("u_ready")
        u_split = sem("u_split")
        dtl_in_psum = sem("dtl_in_psum")
        dtl_ready = sem("dtl_ready")
        dt_raw = sem("dt_raw")
        dt_ready = sem("dt_ready")
        w_ready = sem("w_ready")
        b_in_psum = sem("b_in_psum")
        b_ready = sem("b_ready")
        b_stored = sem("b_stored")
        brow_loaded = [sem(f"brow_loaded{i}") for i in range(DB_RING)]
        c_in_psum = sem("c_in_psum")
        c_ready = sem("c_ready")
        z_in_psum = sem("z_in_psum")
        sz_ready = sem("sz_ready")
        input_done = sem("input_done")
        eps_added = sem("eps_added")
        exp_done = sem("exp_done")
        clamp_done = sem("clamp_done")
        scan_done = sem("scan_done")
        hT_in_psum = sem("hT_in_psum")
        mac_done = sem("mac_done")
        yb_in_psum = sem("yb_in_psum")
        yd_ready = sem("yd_ready")
        yz_ready = sem("yz_ready")
        op_in_psum = sem("op_in_psum")
        x1_ready = sem("x1_ready")
        ln2_stats = sem("ln2_stats")
        ln2_mv = sem("ln2_mv")
        ln2_var = sem("ln2_var")
        ln2_rstd = sem("ln2_rstd")
        xn2_ready = sem("xn2_ready")
        xn2T_in_psum = sem("xn2T_in_psum")
        xn2T_hi_ready = sem("xn2T_hi_ready")
        xn2T_ready = sem("xn2T_ready")
        logit_in_psum = sem("logit_in_psum")
        logit_ready = sem("logit_ready")
        prob_ready = sem("prob_ready")
        route_step = sem("route_step")
        route_ready = sem("route_ready")
        gate_in_psum = sem("gate_in_psum")
        up_in_psum = sem("up_in_psum")
        silu_done = sem("silu_done")
        prod_done = sem("prod_done")
        down_in_psum = sem("down_in_psum")
        net_added = sem("net_added")
        out_stored = [sem(f"out_stored{j}") for j in range(2)]

        mixer_loads = [(win_sb, w_in), (wconv_sb, w_conv), (chan_sb, chan), (wz_sb, w_z),
                       (wdt_sb, w_dt), (wbc_sb, w_bc), (wout_sb, w_out), (wr_sb, w_router),
                       (br_sb, b_router)]
        expert_loads = [(wg_sb, w_gate), (wu_sb, w_up), (wd_sb, w_down)]
        MIXER_LOADED = 16 * len(mixer_loads)
        EXPERTS_LOADED = 16 * len(expert_loads)
        mixer_splits = [(wtap, wtap_s), (wz_sb, wz_s), (wdt_sb, wdt_s), (wbc_sb, wbc_s),
                        (wr_sb, wr_s)]
        expert_splits = [(wg_sb, wg_s), (wu_sb, wu_s)]
        CONSTS = 4 + EXPERTS
        TAP_USES = TAPS // 2

        block = ctx.enter_context(nc.Block())

        @block.sync
        def _(sp):
            sp.dma_start(x_sb[:, 0], x_v[0]).then_inc(x_loaded[0], 16)
            for tile, src in mixer_loads:
                sp.dma_start(tile[:], src).then_inc(mixer_weights, 16)
            for tile, src in expert_loads:
                sp.dma_start(tile[:], src).then_inc(expert_weights, 16)

            def load_x(g, odd):
                at_least(sp, xn_ready, g - 1)
                sp.dma_start(x_sb[:, odd], x_v[bass.ds(g, 1)].rearrange("g p c d -> (g p) c d")
                             ).then_inc(x_loaded[odd], 16)

            def load_row(g, n, odd):
                at_least(sp, input_done, NS * g + n - DB_RING + 1)
                sp.dma_start(brow[:, n % DB_RING], b_rows[odd, n:n + 1].broadcast_to([P, TOK])
                             ).then_inc(brow_loaded[n % DB_RING], 16)

            def step(k, odd, scan, proj, tail, moe):
                G, Q = k + 1, k - 2
                if scan and proj:
                    load_x(k + 1, 1 - odd)
                for s in range(SLOTS):
                    n = s + ROW_LEAD
                    if n == NS and proj:
                        sp.wait_ge(b_ready, G + 1)
                        sp.dma_start(b_rows[1 - odd], b_sb).then_inc(b_stored, 16)
                        wait_apart(sp, b_stored, 16 * (G + 1), sp_passed)
                    if n < NS and scan:
                        load_row(k, n, odd)
                    if n >= NS and proj:
                        load_row(G, n - NS, 1 - odd)
                    if s == 4 and scan:
                        at_least(sp, x1_ready, k)
                        sp.dma_start(res[:], x_v[bass.ds(k, 1)].rearrange("g p c d -> (g p) c d")
                                     ).then_inc(res_loaded, 16)
                if moe:
                    sp.wait_ge(net_added, NETS * (Q + 1))
                    sp.dma_start(out_v[bass.ds(Q, 1)].rearrange("g p c d -> (g p) c d"),
                                 x1[:, odd]).then_inc(out_stored[odd], 16)

            run_steps(sp, step)
            for j in range(2):
                sp.wait_ge(out_stored[j], 16 * (GROUPS // 2))

        @block.gpsimd
        def _(pool):
            pool.memset(ident[:], 0.0).then_inc(ident_set, 1)
            for part in xnT_s:
                pool.memset(part[:].bitcast(F32), 0.0).then_inc(consts, 1)
            pool.memset(ones[:], 1.0).then_inc(consts, 1)
            pool.memset(neg_half[:], -0.5).then_inc(consts, 1)
            for e in range(EXPERTS):
                pool.memset(rank[:, e:e + 1], float(EXPERTS - e)).then_inc(consts, 1)
            pool.wait_ge(ident_set, 1)
            pool.affine_select(out=ident[:], in_=ident[:], compare_op=ALU.not_equal, fill=1.0,
                               base=0, pattern=[[-1, P]], channel_multiplier=1).then_inc(ident_set, 1)
            pool.wait_ge(consts, CONSTS)

            for j, (w, (hi, lo)) in enumerate(mixer_splits):
                pool.wait_ge(mixer_hi, j + 1)
                pool.tensor_tensor(lo[:], w[:], hi[:].bitcast(F32), ALU.subtract).then_inc(mixer_split, 1)
            pool.wait_ge(flag_ready, 2)
            clip_bites = pool.value_load(flag[0:1, 0:1], min_val=0, max_val=1)

            def rstd(g, mv, var_done, mv_done, done, rs):
                wait_apart(pool, mv_done, CHUNKS * (g + 1), pool_passed)
                pool.tensor_scalar(rs[:], mv[:, :, 1], LN_EPS, 1.0, ALU.add, ALU.mult).then_inc(var_done, 1)
                pool.wait_ge(var_done, g + 1)
                pool.tensor_tensor(rs[:], rs[:], neg_half[:], ALU.pow).then_inc(done, 1)

            def clamp(g, n):
                pool.wait_ge(exp_done, 2 * (NS * g + n) + 2)
                pool.sem_inc(pool_passed, 1)
                with pool.If(clip_bites == 1):
                    part = dA[:, n % DA_RING].rearrange("p h (s t) -> p (h s) t", s=SPG)[:, :, 1:]
                    pool.tensor_scalar(part, part, float(np.exp(np.float32(CLIP))),
                                       float(np.exp(np.float32(-CLIP))),
                                       ALU.min, ALU.max).then_inc(clamp_done, 1)
                with pool.Else():
                    pool.sem_inc(clamp_done, 1)

            def state_input(g, n):
                j = NS * g + n
                if n == 0:
                    pool.wait_ge(w_ready, g + 1)
                pool.wait_ge(brow_loaded[n % DB_RING], 16 * (NS // DB_RING * g + n // DB_RING + 1))
                at_least(pool, scan_done, j - DB_RING + 1)
                row = brow[:, n % DB_RING].rearrange("p (o t) -> p o t", o=1).broadcast_to([P, HALVES, TOK])
                pool.tensor_tensor(dB[:, n % DB_RING], w_sb[:], row, ALU.mult).then_inc(input_done, 1)

            def step(k, odd, scan, proj, tail, moe):
                G, M, Q = k + 1, k - 1, k - 2
                for s in range(SLOTS):
                    n = s + CLAMP_LEAD
                    if n < NS and scan:
                        clamp(k, n)
                    if n >= NS and proj:
                        clamp(G, n - NS)
                    n = s + INPUT_LEAD
                    if n < NS and scan:
                        state_input(k, n)
                    if n >= NS and proj:
                        state_input(G, n - NS)
                    if s == 0 and proj:
                        rstd(G, mv1, ln1_var, ln1_mv, ln1_rstd, rstd1)
                    if s in (0, 1) and tail:
                        half = s
                        pool.wait_ge(yd_ready, 2 * M + half + 1)
                        at_least(pool, op_in_psum, M)
                        pool.tensor_tensor(yz[:, half], yz[:, half], sz[:, 1 - odd, half],
                                           ALU.mult).then_inc(yz_ready, 1)
                    if s == 4 and tail:
                        rstd(M, mv2, ln2_var, ln2_mv, ln2_rstd, rstd2)
                    if s in (4, 5) and proj:
                        half = s - 4
                        pool.wait_ge(u_ready, 2 * G + half + 1)
                        at_least(pool, dtl_in_psum, 2 * G)
                        pool.tensor_tensor(u_s[1][:, half], u_sb[:, 1 - odd, half],
                                           u_s[0][:, half].bitcast(F32),
                                           ALU.subtract).then_inc(u_split, 1)
                    if s == 5 and proj and not scan:
                        for j, (w, (hi, lo)) in enumerate(expert_splits):
                            pool.wait_ge(expert_hi, j + 1)
                            pool.tensor_tensor(lo[:], w[:], hi[:].bitcast(F32), ALU.subtract).then_inc(expert_split, 1)
                        pool.wait_ge(expert_split, 2)
                        pool.memset(stage.rearrange("p (q t) -> p q t", t=SEQ)[:, :, 0:1], 0.0).then_inc(starts_zeroed, 1)
                    if s == 12 and proj:
                        pool.wait_ge(dt_ready, G + 1)
                        at_least(pool, input_done, NS * G)
                        pool.tensor_tensor(w_sb[:], dt_sb[:], u_sb[:, 1 - odd],
                                           ALU.mult).then_inc(w_ready, 1)

            run_steps(pool, step)

        @block.scalar
        def _(act):
            act.wait_ge(mixer_weights, MIXER_LOADED)
            act.activation(A_sb[:], chan_sb[:, :, 0:NS], ACT.Exp).then_inc(a_exp, 1)
            act.wait_ge(a_exp, 1)
            act.activation(A_sb[:], A_sb[:], ACT.Copy, scale=-1.0).then_inc(a_ready, 1)
            for j in range(TAP_USES):
                act.wait_ge(tap_in_psum, j + 1)
                act.activation(wtap[:, 2 * j:2 * j + 2], p_misc[:].rearrange("p (k c) -> p k c", k=2),
                               ACT.Copy).then_inc(tap_ready, 1)
            act.wait_ge(tap_ready, TAP_USES)
            for w, (hi, lo) in mixer_splits:
                act.activation(hi[:], w[:], ACT.Copy).then_inc(mixer_hi, 1)
            act.wait_ge(a_ready, 1)
            act.wait_ge(consts, CONSTS)

            def add_eps(g, n):
                j = NS * g + n
                act.wait_ge(input_done, j + 1)
                act.activation(dB[:, n % DB_RING], dB[:, n % DB_RING], ACT.Copy, bias=STATE_EPS
                               ).then_inc(eps_added, 1)

            def decays(g, n):
                if n == 0:
                    act.wait_ge(dt_ready, g + 1)
                    act.wait_ge(starts_zeroed, 1)
                j = NS * g + n
                at_least(act, scan_done, j - DA_RING + 1)
                for half in range(HALVES):
                    src = dt_sb[:, half].rearrange("p (s t) -> p s t", s=SPG)
                    dst = dA[:, n % DA_RING, half].rearrange("p (s t) -> p s t", s=SPG)
                    act.activation(dst[:, :, 1:], src[:, :, 1:], ACT.Exp,
                                   scale=A_sb[:, half, n:n + 1]).then_inc(exp_done, 1)

            def step(k, odd, scan, proj, tail, moe):
                G, M, Q = k + 1, k - 1, k - 2
                def silu(kind, i):
                    if kind == GU:
                        act.wait_ge(gate_in_psum, UNITS * Q + i + 1)
                        at_least(act, down_in_psum, NETS * Q + max(i // 2 - 1, 0))
                        act.activation(hm[:, i // 2 % 2, i % 2], p_gate[i % 2][:], ACT.Silu).then_inc(silu_done, 1)

                for s in range(SLOTS):
                    items = WORK[s] if moe else []
                    n = s + EPS_LEAD
                    if n < NS and scan:
                        add_eps(k, n)
                    if n >= NS and proj:
                        add_eps(G, n - NS)
                    for item in items[:1]:
                        silu(*item)
                    for n in EXP_SLOTS.get(s, ())[:1]:
                        if s < 14 and scan:
                            decays(k, n)
                        if s >= 14 and proj:
                            decays(G, n)
                    if s == 2 and proj:
                        act.wait_ge(xnT_in_psum, G + 1)
                        at_least(act, z_in_psum, 2 * G)
                        act.activation(xnT_s[0][:, :, TAPS - 1:], p_misc[:].rearrange("p (s t) -> p s t", s=SPG),
                                       ACT.Copy).then_inc(xnT_hi_ready, 1)
                    if s in (4, 5) and proj:
                        half = s - 4
                        act.wait_ge(u_in_psum, 2 * G + half + 1)
                        if tail:
                            act.wait_ge(yd_ready, 2 * M + half + 1)
                        act.activation(u_sb[:, 1 - odd, half], p_misc[:], ACT.Identity,
                                       bias=chan_sb[:, half, NS:NS + 1])
                        at_least(act, dtl_in_psum, 2 * G)
                        act.activation(u_s[0][:, half], p_misc[:], ACT.Identity,
                                       bias=chan_sb[:, half, NS:NS + 1]).then_inc(u_ready, 1)
                    if s == 5 and proj and not scan:
                        act.wait_ge(expert_weights, EXPERTS_LOADED)
                        for w, (hi, lo) in expert_splits:
                            act.activation(hi[:], w[:], ACT.Copy).then_inc(expert_hi, 1)
                    if s == 6 and tail:
                        act.wait_ge(xn2T_in_psum, M + 1)
                        at_least(act, up_in_psum, UNITS * (M - 1))
                        act.activation(xn2T_s[1 - odd][0][:], p_misc[:], ACT.Copy).then_inc(xn2T_hi_ready, 1)
                    if s in (7, 8) and proj:
                        half = s - 7
                        act.wait_ge(dtl_in_psum, 2 * G + half + 1)
                        act.activation(dtl[:, half], p_misc[:], ACT.Identity,
                                       bias=chan_sb[:, half, NS + 1:NS + 2]).then_inc(dtl_ready, 1)
                    if s == 9 and tail:
                        act.wait_ge(logit_in_psum, M + 1)
                        act.activation(logit[:], p_misc[:, 0:CHUNKS * EXPERTS].rearrange(
                            "p (c e) -> p c e", c=CHUNKS), ACT.Copy).then_inc(logit_ready, 1)
                    if s == 10 and proj:
                        act.wait_ge(b_in_psum, G + 1)
                        act.activation(b_sb, p_misc[0:NS], ACT.Copy).then_inc(b_ready, 1)
                    if s == 11 and proj:
                        act.wait_ge(c_in_psum, G + 1)
                        if tail:
                            act.wait_ge(mac_done, PAIRS * NS * k)
                        act.activation(c_sb[:, 1 - odd], p_misc[:, 0:CHUNKS * NS].rearrange(
                            "p (c n) -> p c n", c=CHUNKS), ACT.Copy).then_inc(c_ready, 1)
                    for n in EXP_SLOTS.get(s, ())[1:]:
                        if s < 14 and scan:
                            decays(k, n)
                        if s >= 14 and proj:
                            decays(G, n)
                    for item in items[1:2]:
                        silu(*item)
                    if s in (8, 9) and proj:
                        half = s - 8
                        act.wait_ge(z_in_psum, 2 * G + half + 1)
                        if tail:
                            act.wait_ge(yz_ready, 2 * (M + 1))
                        act.activation(sz[:, 1 - odd, half], p_misc[:], ACT.Silu).then_inc(sz_ready, 1)
                    for item in items[2:]:
                        silu(*item)
                    if s == 11 and proj:
                        act.wait_ge(dtl_ready, 2 * (G + 1))
                        if scan:
                            act.wait_ge(exp_done, 2 * NS * G)
                        act.activation(dt_sb[:], dtl[:], ACT.Sigmoid).then_inc(dt_raw, 1)
                    if s == 11 and tail:
                        act.wait_ge(logit_ready, M + 1)
                        at_least(act, route_ready, M)
                        act.activation(prob[:], logit[:], ACT.Sigmoid).then_inc(prob_ready, 1)

            run_steps(act, step)

        @block.tensor
        def _(pe):
            pe.wait_ge(mixer_weights, MIXER_LOADED)
            pe.wait_ge(ident_set, 2)
            pe.wait_ge(consts, CONSTS)
            for j in range(TAP_USES):
                at_least(pe, tap_ready, j)
                for q in range(2):
                    for half in range(HALVES):
                        mm = pe.matmul(p_misc[:, q * CH:(q + 1) * CH], win_sb[:, half],
                                       wconv_sb[:, half, 2 * j + q],
                                       start=half == 0, stop=half == HALVES - 1)
                mm.then_inc(tap_in_psum, 1)
            pe.wait_ge(tap_ready, TAP_USES)
            pe.wait_ge(amin_ready, 1)
            pe.matmul(p_down[0:1, 0], amin[:], ident[:], start=True, stop=True).then_inc(amin_in_psum, 1)

            def states_by_token(g, n):
                j = NS * g + n
                pe.wait_ge(scan_done, j + 1)
                for pair in range(PAIRS):
                    at_least(pe, mac_done, PAIRS * (j - 1) + pair + 1)
                    for c in range(2):
                        for half in range(HALVES):
                            t0 = (2 * pair + c) * P
                            mm = pe.transpose(p_hT[pair][:, c, half * P:(half + 1) * P],
                                              h[:, n % 2, half, t0:t0 + P], ident[:])
                    mm.then_inc(hT_in_psum, 1)

            def split_matmul(out, w, x, start, stop):
                pe.matmul(out, w[0], x[0], start=start, stop=False)
                pe.matmul(out, w[0], x[1], start=False, stop=False)
                return pe.matmul(out, w[1], x[0], start=False, stop=stop)

            def both(parts, *index):
                return tuple(p[index] for p in parts)

            def use_yback(M, half, odd, last):
                pe.wait_ge(mac_done, PAIRS * NS * (M + 1))
                if half == 1:
                    pe.wait_ge(yd_ready, 2 * M + 1)
                elif last:
                    pe.wait_ge(logit_ready, M)
                else:
                    pe.wait_ge(c_ready, M + 2)
                for c in range(CHUNKS):
                    mm = pe.transpose(p_misc[:, c * P:(c + 1) * P],
                                      yT[:, odd, c, half * P:(half + 1) * P], ident[:])
                mm.then_inc(yb_in_psum, 1)

            def use_xnT(G, tail):
                pe.wait_ge(xn_ready, G + 1)
                if tail:
                    pe.wait_ge(yd_ready, 2 * (G - 1))
                else:
                    at_least(pe, c_ready, G)
                for c in range(CHUNKS):
                    mm = pe.transpose(p_misc[:, c * P:(c + 1) * P], xn[:, c], ident[:])
                mm.then_inc(xnT_in_psum, 1)

            def use_outproj(M, proj):
                pe.wait_ge(yz_ready, 2 * (M + 1))
                if proj:
                    pe.wait_ge(xnT_ready, M + 3)
                for c in range(CHUNKS):
                    for half in range(HALVES):
                        mm = pe.matmul(p_misc[:, c * DM:(c + 1) * DM], yz[:, half, c * P:(c + 1) * P],
                                       wout_sb[:, half], start=half == 0, stop=half == HALVES - 1)
                mm.then_inc(op_in_psum, 1)

            def use_u(G, half, tail):
                pe.wait_ge(xnT_ready, G + 1)
                if half == 1:
                    pe.wait_ge(u_ready, 2 * G + 1)
                elif tail:
                    pe.wait_ge(x1_ready, G - 1)
                for t in range(TAPS):
                    mm = split_matmul(p_misc[:].rearrange("p (s t) -> p s t", s=SPG),
                                      both(wtap_s, ALL, t, slice(half * P, (half + 1) * P)),
                                      both(xnT_s, ALL, ALL, slice(t, t + SEQ)),
                                      t == 0, t == TAPS - 1)
                mm.then_inc(u_in_psum, 1)

            def use_xn2T(M, proj):
                pe.wait_ge(xn2_ready, M + 1)
                if proj:
                    pe.wait_ge(u_ready, 2 * (M + 3))
                for c in range(CHUNKS):
                    mm = pe.transpose(p_misc[:, c * P:(c + 1) * P], xn2[:, c], ident[:])
                mm.then_inc(xn2T_in_psum, 1)

            def use_dt(G, half, tail):
                pe.wait_ge(u_split, 2 * (G + 1))
                if half == 1:
                    pe.wait_ge(dtl_ready, 2 * G + 1)
                elif tail:
                    pe.wait_ge(xn2T_ready, G - 1)
                for q in range(HALVES):
                    mm = split_matmul(p_misc[:], both(wdt_s, ALL, q, slice(half * P, (half + 1) * P)),
                                      both(u_s, ALL, q), q == 0, q == HALVES - 1)
                mm.then_inc(dtl_in_psum, 1)

            def use_logit(M, odd, proj):
                pe.wait_ge(xn2T_ready, M + 1)
                if proj:
                    pe.wait_ge(sz_ready, 2 * (M + 2) + 1)
                for c in range(CHUNKS):
                    o = p_misc[:, c * EXPERTS:(c + 1) * EXPERTS]
                    split_matmul(o, both(xn2T_s[odd], ALL, slice(c * P, (c + 1) * P)),
                                 both(wr_s, ALL, ALL), True, False)
                    mm = pe.matmul(o, ones[:], br_sb[:], start=False, stop=True)
                mm.then_inc(logit_in_psum, 1)

            def use_b(G):
                pe.wait_ge(sz_ready, 2 * (G + 1))
                for q in range(HALVES):
                    mm = split_matmul(p_misc[0:NS], both(wbc_s, ALL, q, slice(0, NS)),
                                      both(u_s, ALL, q), q == 0, q == HALVES - 1)
                mm.then_inc(b_in_psum, 1)

            def use_c(G, odd):
                pe.wait_ge(b_ready, G + 1)
                for c in range(CHUNKS):
                    for q in range(HALVES):
                        mm = pe.matmul(p_misc[:, c * NS:(c + 1) * NS], u_sb[:, odd, q, c * P:(c + 1) * P],
                                       wbc_sb[:, q, NS:], start=q == 0, stop=q == HALVES - 1)
                mm.then_inc(c_in_psum, 1)

            def use_z(G, half, tail):
                if half == 0:
                    pe.wait_ge(dtl_ready, 2 * (G + 1))
                elif tail:
                    pe.wait_ge(logit_ready, G - 1)
                else:
                    pe.wait_ge(sz_ready, 2 * G + 1)
                split_matmul(p_misc[:].rearrange("p (s t) -> p s t", s=SPG),
                             both(wz_s, ALL, slice(half * P, (half + 1) * P)),
                             both(xnT_s, ALL, ALL, slice(TAPS - 1, None)),
                             True, True).then_inc(z_in_psum, 1)

            def gate_up(M, i, odd):
                e, half = divmod(i, 2)
                part = ALL, e, slice(half * P, (half + 1) * P)
                if i == 0:
                    pe.wait_ge(xn2T_ready, M + 1)
                at_least(pe, silu_done, UNITS * M + i - 1)
                split_matmul(p_gate[i % 2][:], both(wg_s, *part), both(xn2T_s[odd], ALL),
                             True, True).then_inc(gate_in_psum, 1)
                at_least(pe, prod_done, UNITS * M + i - 1)
                split_matmul(p_up[i % 2][:], both(wu_s, *part), both(xn2T_s[odd], ALL),
                             True, True).then_inc(up_in_psum, 1)

            def down(M, e):
                pe.wait_ge(prod_done, UNITS * M + 2 * e + 2)
                at_least(pe, net_added, NETS * M + e)
                for c in range(CHUNKS):
                    for half in range(2):
                        mm = pe.matmul(p_down[:, c], hm[:, e % 2, half, c * P:(c + 1) * P],
                                       wd_sb[:, e, half], start=half == 0, stop=half == 1)
                mm.then_inc(down_in_psum, 1)

            def step(k, odd, scan, proj, tail, moe):
                G, M, Q = k + 1, k - 1, k - 2

                def work(kind, i):
                    if kind == GU:
                        gate_up(Q, i, odd)
                    else:
                        down(Q, i)

                for s in range(SLOTS):
                    items = WORK[s] if moe else []
                    for item in items[:1]:
                        work(*item)
                    if s in (0, 1) and tail:
                        use_yback(M, s, 1 - odd, isinstance(k, int) and k == GROUPS)
                    if s == 2 and proj:
                        use_xnT(G, tail)
                    if s == 3 and tail:
                        use_outproj(M, proj)
                    if s in (4, 5) and proj:
                        use_u(G, s - 4, tail)
                    if s == 6 and tail:
                        use_xn2T(M, proj)
                    if s in (7, 8) and proj:
                        use_dt(G, s - 7, tail)
                    if s == 9 and tail:
                        use_logit(M, 1 - odd, proj)
                    if s == 10 and proj:
                        use_b(G)
                    if s == 11 and proj:
                        use_c(G, 1 - odd)
                    for item in items[1:2]:
                        work(*item)
                    if s in (8, 9) and proj:
                        use_z(G, s - 8, tail)
                    for item in items[2:]:
                        work(*item)
                    if scan:
                        states_by_token(k, s)

            pe.wait_ge(mixer_split, len(mixer_splits))
            run_steps(pe, step)

        @block.vector
        def _(dve):
            dve.wait_ge(consts, CONSTS)
            dve.wait_ge(a_ready, 1)
            dve.tensor_reduce(amin[:], A_sb[:].rearrange("p h n -> p (h n)"), AX.X, ALU.min).then_inc(amin_ready, 1)
            dve.wait_ge(amin_in_psum, 1)
            dve.tensor_reduce(amin_all[:], p_down[0:1, 0], AX.X, ALU.min).then_inc(flag_ready, 1)
            dve.wait_ge(flag_ready, 1)
            dve.tensor_scalar(flag[:], amin_all[:], -CLIP, None, ALU.is_lt).then_inc(flag_ready, 1)

            def scan_state(g, n):
                j = NS * g + n
                at_least(dve, hT_in_psum, PAIRS * (j - 1))
                dve.wait_ge(eps_added, j + 1)
                dve.wait_ge(clamp_done, j + 1)
                flat = "p h t -> p (h t)"
                dve.tensor_tensor_scan(h[:, n % 2].rearrange(flat), dA[:, n % DA_RING].rearrange(flat),
                                       dB[:, n % DB_RING].rearrange(flat), 0.0,
                                       ALU.mult, ALU.add).then_inc(scan_done, 1)

            def sum_states(g, n, odd):
                j = NS * g + n
                for pair in range(PAIRS):
                    dve.wait_ge(hT_in_psum, PAIRS * j + pair + 1)
                    if n == 0 and pair == 0:
                        dve.wait_ge(c_ready, g + 1)
                        at_least(dve, yb_in_psum, 2 * (g - 1))
                    at_least(dve, mac_done, PAIRS * (j - 1) + pair + 1)
                    for c in range(2):
                        cc = 2 * pair + c
                        scalar = c_sb[:, odd, cc, n:n + 1]
                        if n == 0:
                            op = dve.tensor_scalar(yT[:, odd, cc], p_hT[pair][:, c], scalar, None, ALU.mult)
                        else:
                            op = dve.scalar_tensor_tensor(yT[:, odd, cc], p_hT[pair][:, c], scalar,
                                                          yT[:, odd, cc], ALU.mult, ALU.add)
                    op.then_inc(mac_done, 1)

            def norm_stats(g, src, stats, mv, stats_done, mv_done):
                for c in range(CHUNKS):
                    dve.bn_stats(stats[:, c], src[:, c]).then_inc(stats_done, 1)
                wait_apart(dve, stats_done, CHUNKS * (g + 1), dve_passed)
                for c in range(CHUNKS):
                    dve.bn_aggr(mv[:, c], stats[:, c]).then_inc(mv_done, 1)

            def norm_apply(dst, src, mv, rs, done):
                for c in range(CHUNKS):
                    op = dve.tensor_scalar(dst[:, c], src[:, c], mv[:, c, 0:1], rs[:, c:c + 1],
                                           ALU.subtract, ALU.mult)
                op.then_inc(done, 1)

            def pick_experts(M, odd):
                dve.wait_ge(prob_ready, M + 1)
                wide = [P, CHUNKS, EXPERTS]
                rank_b = rank[:].rearrange("p (o e) -> p o e", o=1).broadcast_to(wide)

                def spread(v):
                    return v[:].rearrange("p (c o) -> p c o", o=1).broadcast_to(wide)

                count = [0]

                def then(op):
                    count[0] += 1
                    op.then_inc(route_step, 1)
                    dve.wait_ge(route_step, ROUTE_STEPS * M + count[0])

                src = prob
                for j in range(2):
                    then(dve.tensor_reduce(top[j][:], src[:], AX.X, ALU.max))
                    then(dve.tensor_tensor(key[:], src[:], spread(top[j]), ALU.is_equal))
                    then(dve.tensor_tensor(key[:], key[:], rank_b, ALU.mult))
                    then(dve.tensor_reduce(win[:], key[:], AX.X, ALU.max))
                    then(dve.tensor_tensor(hit[j][:], key[:], spread(win), ALU.is_equal))
                    if j == 0:
                        then(dve.scalar_tensor_tensor(rest[:], hit[0][:], -2.0, prob[:], ALU.mult, ALU.add))
                        src = rest
                then(dve.tensor_tensor(win[:], top[0][:], top[1][:], ALU.add))
                then(dve.reciprocal(share[:], win[:]))
                then(dve.tensor_tensor(key[:], hit[0][:], hit[1][:], ALU.add))
                op = dve.tensor_tensor(key[:], key[:], spread(share), ALU.mult)
                then(op)
                assert count[0] == ROUTE_STEPS
                dve.tensor_tensor(route[:, odd], key[:], prob[:], ALU.mult).then_inc(route_ready, 1)

            def product(M, i):
                e, half = divmod(i, 2)
                dve.wait_ge(silu_done, UNITS * M + i + 1)
                dve.wait_ge(up_in_psum, UNITS * M + i + 1)
                dve.tensor_tensor(hm[:, e % 2, half], p_up[i % 2][:], hm[:, e % 2, half], ALU.mult).then_inc(prod_done, 1)

            def add_net(M, e, odd):
                dve.wait_ge(down_in_psum, NETS * M + e + 1)
                at_least(dve, net_added, NETS * M + e)
                if e == 0:
                    dve.tensor_tensor(x1[:, odd], p_down[:], x1[:, odd], ALU.add).then_inc(net_added, 1)
                    return
                if e == 1:
                    dve.wait_ge(route_ready, M + 1)
                for c in range(CHUNKS):
                    op = dve.scalar_tensor_tensor(x1[:, odd, c], p_down[:, c], route[:, odd, c, e - 1:e],
                                                  x1[:, odd, c], ALU.mult, ALU.add)
                op.then_inc(net_added, 1)

            def step(k, odd, scan, proj, tail, moe):
                G, M, Q = k + 1, k - 1, k - 2
                for s in range(SLOTS):
                    items = WORK[s] if moe else []
                    if scan:
                        scan_state(k, s)
                    if s > 0 and scan:
                        sum_states(k, s - 1, odd)
                    if s == 0 and tail:
                        sum_states(M, NS - 1, 1 - odd)
                    for kind, i in items[:1]:
                        if kind == GU:
                            product(Q, i)
                    if s == 0 and proj:
                        dve.wait_ge(x_loaded[1 - odd], transfers(G, 1 - odd))
                        at_least(dve, ln1_rstd, G)
                        norm_stats(G, x_sb[:, 1 - odd], stats1, mv1, ln1_stats, ln1_mv)
                    if s == 1 and proj:
                        dve.wait_ge(ln1_rstd, G + 1)
                        at_least(dve, xnT_in_psum, G)
                        at_least(dve, b_stored, 16 * G)
                        if tail:
                            at_least(dve, xn2T_in_psum, M)
                        norm_apply(xn, x_sb[:, 1 - odd], mv1, rstd1, xn_ready)
                    if s in (0, 1) and tail:
                        half = s
                        dve.wait_ge(yb_in_psum, 2 * M + half + 1)
                        at_least(dve, yz_ready, 2 * M)
                        dve.scalar_tensor_tensor(yz[:, half], u_sb[:, 1 - odd, half],
                                                 chan_sb[:, half, NS + 2:NS + 3], p_misc[:],
                                                 ALU.mult, ALU.add).then_inc(yd_ready, 1)
                    if s == 2 and proj:
                        dve.wait_ge(xnT_hi_ready, G + 1)
                        dve.tensor_tensor(xnT_s[1][:, :, TAPS - 1:], p_misc[:].rearrange("p (s t) -> p s t", s=SPG),
                                          xnT_s[0][:, :, TAPS - 1:].bitcast(F32),
                                          ALU.subtract).then_inc(xnT_ready, 1)
                    if s == 3 and tail:
                        dve.wait_ge(op_in_psum, M + 1)
                        dve.wait_ge(res_loaded, 16 * (M + 1))
                        at_least(dve, out_stored[1 - odd], transfers(M, 1 - odd) - 16)
                        dve.tensor_tensor(x1[:, 1 - odd], p_misc[:].rearrange("p (c d) -> p c d", c=CHUNKS),
                                          res[:], ALU.add).then_inc(x1_ready, 1)
                    if s == 4 and tail:
                        dve.wait_ge(x1_ready, M + 1)
                        at_least(dve, ln2_rstd, M)
                        norm_stats(M, x1[:, 1 - odd], stats2, mv2, ln2_stats, ln2_mv)
                    if s == 5 and tail:
                        dve.wait_ge(ln2_rstd, M + 1)
                        at_least(dve, xn2T_in_psum, M)
                        if proj:
                            dve.wait_ge(xnT_in_psum, G + 1)
                        norm_apply(xn2, x1[:, 1 - odd], mv2, rstd2, xn2_ready)
                    if s == 6 and tail:
                        dve.wait_ge(xn2T_hi_ready, M + 1)
                        dve.tensor_tensor(xn2T_s[1 - odd][1][:], p_misc[:], xn2T_s[1 - odd][0][:].bitcast(F32),
                                          ALU.subtract).then_inc(xn2T_ready, 1)
                    if s == 12 and proj:
                        dve.wait_ge(dt_raw, G + 1)
                        dve.tensor_scalar(dt_sb[:], dt_sb[:], DT_MIN, 1.0,
                                          ALU.max, ALU.min).then_inc(dt_ready, 1)
                    for kind, i in items[1:]:
                        if kind == GU:
                            product(Q, i)
                    for kind, e in items:
                        if kind == DN:
                            add_net(Q, e, odd)
                    if s == 12 and tail:
                        pick_experts(M, 1 - odd)

            run_steps(dve, step)


_OUT = "out_dram"


def kernel(**inputs):
    import concourse.bacc as bacc
    from concourse.bass_utils import run_bass_kernel_spmd

    a = {n: np.asarray(v) for n, v in inputs.items()}
    x = a["L0_attn_x"]

    def parts(m):
        return m.reshape((m.shape[0] // P, P) + m.shape[1:]).swapaxes(0, 1)

    w_in = a["L0_attn_in_proj_w"]
    gates = np.concatenate([a["L0_ffn_sg_w"][None], a["L0_ffn_wg"]])
    ups = np.concatenate([a["L0_ffn_su_w"][None], a["L0_ffn_wu"]])
    downs = np.concatenate([a["L0_ffn_sd_w"][None], a["L0_ffn_wd"]])
    arrays = {
        "x": x.reshape(TOKENS, DM),
        "w_in": parts(w_in[:CH]),
        "w_z": w_in[CH:].T,
        "w_conv": parts(a["L0_attn_conv_w"].transpose(1, 2, 0)),
        "w_dt": parts(a["L0_attn_dt_w"].T),
        "w_bc": parts(np.concatenate([a["L0_attn_B_w"], a["L0_attn_C_w"]]).T),
        "w_out": parts(a["L0_attn_out_w"].T),
        "chan": parts(np.concatenate([a["L0_attn_A_log"], a["L0_attn_conv_b"][:, None],
                                      a["L0_attn_dt_b"][:, None], a["L0_attn_D"][:, None]], axis=1)),
        "w_router": a["L0_ffn_router_w"].T,
        "b_router": a["L0_ffn_routing_bias"][None],
        "w_gate": gates.transpose(2, 0, 1),
        "w_up": ups.transpose(2, 0, 1),
        "w_down": downs.transpose(2, 0, 1).reshape(2, P, NETS, DM).transpose(1, 2, 0, 3),
    }
    nc = bacc.Bacc("TRN2", target_bir_lowering=False, num_devices=1)
    feed, args = {}, []
    for name, arr in arrays.items():
        arr = np.ascontiguousarray(arr)
        feed[f"{name}_dram"] = arr
        args.append(nc.dram_tensor(f"{name}_dram", arr.shape, mybir.dt.from_np(arr.dtype),
                                   kind="ExternalInput").ap())
    out = nc.dram_tensor(_OUT, (TOKENS, DM), F32, kind="ExternalOutput").ap()
    b_rows = nc.dram_tensor("b_rows_dram", (2, NS, TOK), F32, kind="Internal").ap()
    build(nc, *args, b_rows, out)
    r = run_bass_kernel_spmd(nc, [feed], core_ids=[0])
    return r.results[0][_OUT].reshape(x.shape)
```

```python
from contextlib import ExitStack

import numpy as np
import concourse.bass as bass
from concourse import mybir

F32 = mybir.dt.float32
F32R = mybir.dt.float32r
ALU = mybir.AluOpType
ACT = mybir.ActivationFunctionType
AX = mybir.AxisListType

P = 128
DM = 128
CH = 256
HALVES = CH // P
NS = 16
TAPS = 4
SEQ = 256
TOKENS = 32 * SEQ
TOK = 512
SPG = TOK // SEQ
CHUNKS = TOK // P
PAIRS = CHUNKS // 2
GROUPS = TOKENS // TOK
SLOTS = NS
EXPERTS = 8
NETS = EXPERTS + 1
HID = 256
UNITS = 2 * NETS
LN_EPS = 1e-5
STATE_EPS = 1e-6
CLIP = 5.0
DT_MIN = 1e-4
DA_RING = 8
DB_RING = 4
DECAY_LEAD = 4
CLAMP_LEAD, EPS_LEAD, INPUT_LEAD, ROW_LEAD = 1, 2, 3, 5
ROUTE_STEPS = 15
ALL = slice(None)


PE_ORDER = ("wwmh mwmh wwmh wmwh wh wwwh mwmh wmwmh wmh wmwmh mwmh wwh wh wwwwh wh wh")
WORK = "G0 G1 G2 G3 D0 D1 G4 G5 G6 G7 G8 D2 D3 G9 G10 G11 G12 D4 G13 D5 G14 G15 D6 G16 G17 D7 D8"
MISC_USES = "yb0 yb1 xnT op u0 u1 xn2T dt0 dt1 z0 logit z1 bc c"
ACT_ORDER = ("gg eg egmx exd exxdm egg egdggx em emxxmd exmgmg emggmxd em exxxmmdmggg e ed eggxdxx exd")
ACT_WORK = "xnT u0 u1 xn2T dt0 dt1 z0 logit z1 bc c sigmoid_dt sigmoid_router"
DVE_ORDER = ("sypmm smmypp smpya smmy say sppypp s sympam syayppy s sypa sp syaymp spypa spypaa smym")
DVE_WORK = "stats1 yd0 xn yd1 xnT_lo x1 stats2 xn2 xn2T_lo clip_dt pick0 pick1"


POOL_NETS = "1 6 8"
POOL_ORDER = ("c im i imcmca icamc icm i iccam i iacc ic ica ia iccm i iac iaca")
POOL_WORK = "rstd1 gate0 gate1 u_lo0 rstd2 u_lo1 w"
HM_RING = 3


def at_least(eng, sem, value):
    if isinstance(value, int) and value <= 0:
        return
    eng.wait_ge(sem, value)


def wait_apart(eng, sem, value, passed):
    if isinstance(value, int) and value <= 0:
        return
    eng.wait_ge(sem, value)
    if not isinstance(value, int):
        eng.sem_inc(passed, 1)


def transfers(g, odd):
    return 8 * (g - odd) + 16


def run_steps(eng, step):
    step(-1, 1, False, True, False, False)
    step(0, 0, True, True, False, False)
    step(1, 1, True, True, True, False)
    step(2, 0, True, True, True, True)
    with eng.Fori(0, GROUPS // 2 - 2) as pair:
        step(2 * pair + 3, 1, True, True, True, True)
        step(2 * pair + 4, 0, True, True, True, True)
    step(GROUPS - 1, 1, True, False, True, True)
    step(GROUPS, 0, False, False, True, True)
    step(GROUPS + 1, 1, False, False, False, True)


def build(nc, x, w_in, w_z, w_conv, w_dt, w_bc, w_out, chan, w_router, b_router,
          w_gate, w_up, w_down, b_rows, out):
    x_v = x.rearrange("(g c p) d -> g p c d", c=CHUNKS, p=P)
    out_v = out.rearrange("(g c p) d -> g p c d", c=CHUNKS, p=P)

    ctx = ExitStack()
    with ctx:
        def sb(name, shape, dtype=F32):
            return ctx.enter_context(nc.sbuf_tensor(name, shape, dtype))

        def sb_split(name, shape):
            return sb(f"{name}_hi", shape, F32R), sb(f"{name}_lo", shape, F32R)

        def pb(name, shape):
            return ctx.enter_context(nc.psum_tensor(name, shape, F32))

        def sem(name):
            return ctx.enter_context(nc.semaphore(name))

        ident = sb("ident", [P, P])
        wz_s = sb_split("wz_s", [P, CH])
        wtap_s = sb_split("wtap_s", [P, TAPS, CH])
        wdt_s = sb_split("wdt_s", [P, HALVES, CH])
        wout_sb = sb("wout_sb", [P, HALVES, DM])
        chan_sb = sb("chan_sb", [P, HALVES, NS + 3])
        A_sb = sb("A_sb", [P, HALVES, NS])
        wbc_s = sb_split("wbc_s", [P, HALVES, 2 * NS])
        wr_s = sb_split("wr_s", [P, EXPERTS])
        br_sb = sb("br_sb", [1, EXPERTS])
        ones = sb("ones", [1, P])
        rank = sb("rank", [P, EXPERTS])
        neg_half = sb("neg_half", [P, CHUNKS])
        wg_s = sb_split("wg_s", [P, NETS, HID])
        wu_s = sb_split("wu_s", [P, NETS, HID])
        wd_sb = sb("wd_sb", [P, NETS, 2, DM])

        amin = sb("amin", [P, 1])
        amin_all = sb("amin_all", [1, 1])
        flag = ctx.enter_context(nc.sbuf_tensor("flag", [1, 1], mybir.dt.int32))

        x_sb = sb("x_sb", [P, 2, CHUNKS, DM])
        stats = sb("stats", [P, CHUNKS, 6])
        mv1 = sb("mv1", [P, CHUNKS, 2])
        rstd1 = sb("rstd1", [P, CHUNKS])
        xn = sb("xn", [P, CHUNKS, DM])
        xnT_s = sb_split("xnT_s", [P, SPG, TAPS - 1 + SEQ])
        u_sb = sb("u_sb", [P, 2, HALVES, TOK])
        u_s = sb_split("u_s", [P, HALVES, TOK])
        turns = sb("turns", [P, HALVES, TOK])
        yz = dtl = turns
        dt_sb = sb("dt_sb", [P, HALVES, TOK])
        w_sb = sb("w_sb", [P, HALVES, TOK])
        c_sb = sb("c_sb", [P, 2, CHUNKS, NS])
        brow = sb("brow", [P, DB_RING, TOK])
        sz = sb("sz", [P, 2, HALVES, TOK])
        dA = sb("dA", [P, DA_RING, HALVES, TOK])
        stage = dA[:].rearrange("p n h t -> p (n h t)")
        wg_sb = stage[:, 0:NETS * HID].rearrange("p (e i) -> p e i", e=NETS)
        wu_sb = stage[:, NETS * HID:2 * NETS * HID].rearrange("p (e i) -> p e i", e=NETS)
        wconv_sb = stage[:, 2 * NETS * HID:2 * NETS * HID + HALVES * TAPS * CH].rearrange(
            "p (h k c) -> p h k c", h=HALVES, k=TAPS)
        dB = sb("dB", [P, DB_RING, HALVES, TOK])
        stage_b = dB[:].rearrange("p n h t -> p (n h t)")

        def staged(at, n):
            return stage_b[:, at:at + n]

        wz_sb = staged(TAPS * CH, CH)
        wdt_sb = staged((TAPS + 1) * CH, HALVES * CH).rearrange("p (h c) -> p h c", h=HALVES)
        win_sb = staged((TAPS + 3) * CH, HALVES * DM).rearrange("p (h d) -> p h d", h=HALVES)
        wbc_sb = staged((TAPS + 3) * CH + HALVES * DM, HALVES * 2 * NS).rearrange("p (h n) -> p h n", h=HALVES)
        wr_sb = staged((TAPS + 4) * CH + HALVES * DM, EXPERTS)
        h = sb("h", [P, 2, HALVES, TOK])
        yT = sb("yT", [P, CHUNKS, CH])
        scaled = sb("scaled", [P, 2, CHUNKS, DM])
        res = sb("res", [P, CHUNKS, DM])
        x1 = sb("x1", [P, 2, CHUNKS, DM])
        mv2 = sb("mv2", [P, CHUNKS, 2])
        rstd2 = sb("rstd2", [P, CHUNKS])
        xn2 = xn
        bc_sb = xn[0:2 * NS].rearrange("p c d -> p (c d)")
        xn2T_s = [sb_split(f"xn2T_s{j}", [P, TOK]) for j in range(2)]
        logit = sb("logit", [P, CHUNKS, EXPERTS])
        prob = sb("prob", [P, CHUNKS, EXPERTS])
        hit = [sb(f"hit{j}", [P, CHUNKS, EXPERTS]) for j in range(2)]
        key = sb("key", [P, CHUNKS, EXPERTS])
        rest = logit
        top = [sb(f"top{j}", [P, CHUNKS]) for j in range(2)]
        win = sb("win", [P, CHUNKS])
        share = sb("share", [P, CHUNKS])
        route = sb("route", [P, 2, CHUNKS, EXPERTS])
        hm = sb("hm", [P, HM_RING, 2, TOK])

        p_hT = [pb(f"p_hT{i}", [P, 2, CH]) for i in range(PAIRS)]
        p_gate = [pb(f"p_gate{i}", [P, TOK]) for i in range(2)]
        p_up = [pb(f"p_up{i}", [P, TOK]) for i in range(2)]
        p_down = pb("p_down", [P, CHUNKS, DM])
        p_misc = pb("p_misc", [P, TOK])

        tap_weights = sem("tap_weights")
        mixer_weights = sem("mixer_weights")
        expert_weights = sem("expert_weights")
        consts = sem("consts")
        pool_passed = sem("pool_passed")
        sp_passed = sem("sp_passed")
        dve_passed = sem("dve_passed")
        ident_set = sem("ident_set")
        a_exp = sem("a_exp")
        a_ready = sem("a_ready")
        amin_ready = sem("amin_ready")
        amin_in_psum = sem("amin_in_psum")
        flag_ready = sem("flag_ready")
        tap_in_psum = sem("tap_in_psum")
        tap_hi = sem("tap_hi")
        tap_split = sem("tap_split")
        mixer_hi = sem("mixer_hi")
        mixer_split = sem("mixer_split")
        starts_zeroed = sem("starts_zeroed")
        expert_hi = sem("expert_hi")
        expert_split = sem("expert_split")
        net_scaled = sem("net_scaled")
        x_loaded = [sem(f"x_loaded{j}") for j in range(2)]
        res_loaded = sem("res_loaded")
        ln1_stats = sem("ln1_stats")
        ln1_mv = sem("ln1_mv")
        ln1_var = sem("ln1_var")
        ln1_rstd = sem("ln1_rstd")
        xn_ready = sem("xn_ready")
        xnT_in_psum = sem("xnT_in_psum")
        xnT_hi_ready = sem("xnT_hi_ready")
        xnT_ready = sem("xnT_ready")
        u_in_psum = sem("u_in_psum")
        u_ready = sem("u_ready")
        u_split = sem("u_split")
        dtl_in_psum = sem("dtl_in_psum")
        dtl_ready = sem("dtl_ready")
        dt_raw = sem("dt_raw")
        dt_ready = sem("dt_ready")
        w_ready = sem("w_ready")
        bc_in_psum = sem("bc_in_psum")
        bc_ready = sem("bc_ready")
        b_stored = sem("b_stored")
        brow_loaded = [sem(f"brow_loaded{i}") for i in range(DB_RING)]
        c_in_psum = sem("c_in_psum")
        c_ready = sem("c_ready")
        z_in_psum = sem("z_in_psum")
        sz_ready = sem("sz_ready")
        input_done = sem("input_done")
        eps_added = sem("eps_added")
        exp_done = sem("exp_done")
        clamp_done = sem("clamp_done")
        scan_done = sem("scan_done")
        hT_in_psum = sem("hT_in_psum")
        mac_done = sem("mac_done")
        yb_in_psum = sem("yb_in_psum")
        yd_ready = sem("yd_ready")
        yz_ready = sem("yz_ready")
        op_in_psum = sem("op_in_psum")
        x1_ready = sem("x1_ready")
        ln2_stats = sem("ln2_stats")
        ln2_mv = sem("ln2_mv")
        ln2_var = sem("ln2_var")
        ln2_rstd = sem("ln2_rstd")
        xn2_ready = sem("xn2_ready")
        xn2T_in_psum = sem("xn2T_in_psum")
        xn2T_hi_ready = sem("xn2T_hi_ready")
        xn2T_ready = sem("xn2T_ready")
        logit_in_psum = sem("logit_in_psum")
        logit_ready = sem("logit_ready")
        prob_ready = sem("prob_ready")
        route_step = sem("route_step")
        route_ready = sem("route_ready")
        gate_in_psum = sem("gate_in_psum")
        up_in_psum = sem("up_in_psum")
        silu_done = sem("silu_done")
        prod_done = sem("prod_done")
        down_in_psum = sem("down_in_psum")
        net_added = sem("net_added")
        out_stored = [sem(f"out_stored{j}") for j in range(2)]

        tap_loads = [(win_sb, w_in), (wconv_sb, w_conv)]
        mixer_loads = [(chan_sb, chan), (wz_sb, w_z),
                       (wdt_sb, w_dt), (wbc_sb, w_bc), (wout_sb, w_out), (wr_sb, w_router),
                       (br_sb, b_router)]
        expert_loads = [(wg_sb, w_gate), (wu_sb, w_up), (wd_sb, w_down)]
        MIXER_LOADED = 16 * len(mixer_loads)
        EXPERTS_LOADED = 16 * len(expert_loads)
        mixer_splits = [(wz_sb, wz_s), (wdt_sb, wdt_s), (wbc_sb, wbc_s),
                        (wr_sb, wr_s)]
        expert_splits = [(wg_sb, wg_s), (wu_sb, wu_s)]
        pool_nets = [int(e) for e in POOL_NETS.split()]
        CONSTS = 4 + EXPERTS
        TAP_USES = TAPS // 2

        block = ctx.enter_context(nc.Block())

        @block.sync
        def _(sp):
            for tile, src in tap_loads:
                sp.dma_start(tile[:], src).then_inc(tap_weights, 16)
            sp.dma_start(x_sb[:, 0], x_v[0]).then_inc(x_loaded[0], 16)
            for tile, src in mixer_loads:
                sp.dma_start(tile[:], src).then_inc(mixer_weights, 16)
            for tile, src in expert_loads:
                sp.dma_start(tile[:], src).then_inc(expert_weights, 16)

            def load_x(g, odd):
                at_least(sp, xn_ready, g - 1)
                sp.dma_start(x_sb[:, odd], x_v[bass.ds(g, 1)].rearrange("g p c d -> (g p) c d")
                             ).then_inc(x_loaded[odd], 16)

            def load_row(g, n, odd):
                at_least(sp, input_done, NS * g + n - DB_RING + 1)
                sp.dma_start(brow[:, n % DB_RING], b_rows[odd, n:n + 1].broadcast_to([P, TOK])
                             ).then_inc(brow_loaded[n % DB_RING], 16)

            def step(k, odd, scan, proj, tail, moe):
                G, Q = k + 1, k - 2
                if scan and proj:
                    load_x(k + 1, 1 - odd)
                for s in range(SLOTS):
                    n = s + ROW_LEAD
                    if n == NS and proj:
                        sp.wait_ge(bc_ready, G + 1)
                        sp.dma_start(b_rows[1 - odd], bc_sb[0:NS]).then_inc(b_stored, 16)
                        wait_apart(sp, b_stored, 16 * (G + 1), sp_passed)
                    if n < NS and scan:
                        load_row(k, n, odd)
                    if n >= NS and proj:
                        load_row(G, n - NS, 1 - odd)
                    if s == 4 and scan:
                        at_least(sp, x1_ready, k)
                        sp.dma_start(res[:], x_v[bass.ds(k, 1)].rearrange("g p c d -> (g p) c d")
                                     ).then_inc(res_loaded, 16)
                if moe:
                    sp.wait_ge(net_added, NETS * (Q + 1))
                    sp.dma_start(out_v[bass.ds(Q, 1)].rearrange("g p c d -> (g p) c d"),
                                 x1[:, odd]).then_inc(out_stored[odd], 16)

            run_steps(sp, step)
            for j in range(2):
                sp.wait_ge(out_stored[j], 16 * (GROUPS // 2))

        @block.gpsimd
        def _(pool):
            pool.memset(ident[:], 0.0).then_inc(ident_set, 1)
            for part in xnT_s:
                pool.memset(part[:].bitcast(F32), 0.0).then_inc(consts, 1)
            pool.memset(ones[:], 1.0).then_inc(consts, 1)
            pool.memset(neg_half[:], -0.5).then_inc(consts, 1)
            for e in range(EXPERTS):
                pool.memset(rank[:, e:e + 1], float(EXPERTS - e)).then_inc(consts, 1)
            pool.wait_ge(ident_set, 1)
            pool.affine_select(out=ident[:], in_=ident[:], compare_op=ALU.not_equal, fill=1.0,
                               base=0, pattern=[[-1, P]], channel_multiplier=1).then_inc(ident_set, 1)
            pool.wait_ge(consts, CONSTS)
            pool.wait_ge(flag_ready, 2)
            clip_bites = pool.value_load(flag[0:1, 0:1], min_val=0, max_val=1)

            def rstd(g, mv, var_done, mv_done, done, rs):
                wait_apart(pool, mv_done, CHUNKS * (g + 1), pool_passed)
                pool.tensor_scalar(rs[:], mv[:, :, 1], LN_EPS, 1.0, ALU.add, ALU.mult).then_inc(var_done, 1)
                pool.wait_ge(var_done, g + 1)
                pool.tensor_tensor(rs[:], rs[:], neg_half[:], ALU.pow).then_inc(done, 1)

            def clamp(g, n):
                pool.wait_ge(exp_done, 2 * (NS * g + n) + 2)
                pool.sem_inc(pool_passed, 1)
                with pool.If(clip_bites == 1):
                    part = dA[:, n % DA_RING].rearrange("p h (s t) -> p (h s) t", s=SPG)[:, :, 1:]
                    pool.tensor_scalar(part, part, float(np.exp(np.float32(CLIP))),
                                       float(np.exp(np.float32(-CLIP))),
                                       ALU.min, ALU.max).then_inc(clamp_done, 1)
                with pool.Else():
                    pool.sem_inc(clamp_done, 1)

            def state_input(g, n):
                j = NS * g + n
                if n == 0:
                    pool.wait_ge(w_ready, g + 1)
                pool.wait_ge(brow_loaded[n % DB_RING], 16 * (NS // DB_RING * g + n // DB_RING + 1))
                at_least(pool, scan_done, j - DB_RING + 1)
                row = brow[:, n % DB_RING].rearrange("p (o t) -> p o t", o=1).broadcast_to([P, HALVES, TOK])
                pool.tensor_tensor(dB[:, n % DB_RING], w_sb[:], row, ALU.mult).then_inc(input_done, 1)

            def other_work(kind, k, odd, scan, proj, tail, moe):
                G, M = k + 1, k - 1
                if kind == "rstd1" and proj:
                    rstd(G, mv1, ln1_var, ln1_mv, ln1_rstd, rstd1)
                if kind == "rstd2" and tail:
                    rstd(M, mv2, ln2_var, ln2_mv, ln2_rstd, rstd2)
                if kind in ("gate0", "gate1") and tail:
                    half = int(kind[4])
                    pool.wait_ge(yd_ready, 2 * M + half + 1)
                    at_least(pool, op_in_psum, M)
                    pool.tensor_tensor(yz[:, half], yz[:, half], sz[:, 1 - odd, half],
                                       ALU.mult).then_inc(yz_ready, 1)
                if kind in ("u_lo0", "u_lo1") and proj:
                    half = int(kind[4])
                    pool.wait_ge(u_ready, 2 * G + half + 1)
                    at_least(pool, bc_in_psum, G)
                    pool.tensor_tensor(u_s[1][:, half], u_sb[:, 1 - odd, half],
                                       u_s[0][:, half].bitcast(F32),
                                       ALU.subtract).then_inc(u_split, 1)
                if kind == "u_lo1" and proj and not scan:
                    pool.wait_ge(expert_split, 2)
                    pool.memset(stage.rearrange("p (q t) -> p q t", t=SEQ)[:, :, 0:1], 0.0).then_inc(starts_zeroed, 1)
                if kind == "w" and proj:
                    pool.wait_ge(dt_ready, G + 1)
                    at_least(pool, input_done, NS * G)
                    pool.tensor_tensor(w_sb[:], dt_sb[:], u_sb[:, 1 - odd], ALU.mult).then_inc(w_ready, 1)

            def step(k, odd, scan, proj, tail, moe):
                done = {kind: 0 for kind in "cima"}
                for kind in POOL_ORDER.replace(" ", ""):
                    i = done[kind]
                    done[kind] += 1
                    if kind in "ci":
                        work = clamp if kind == "c" else state_input
                        n = i + (CLAMP_LEAD if kind == "c" else INPUT_LEAD)
                        if n < NS and scan:
                            work(k, n)
                        if n >= NS and proj:
                            work(k + 1, n - NS)
                    if kind == "a" and moe and i in pool_nets:
                        pool.wait_ge(net_scaled, len(pool_nets) * (k - 2) + pool_nets.index(i) + 1)
                        pool.wait_ge(net_added, NETS * (k - 2) + i)
                        pool.tensor_tensor(x1[:, odd], scaled[:, pool_nets.index(i) % 2], x1[:, odd],
                                           ALU.add).then_inc(net_added, 1)
                    if kind == "m":
                        other_work(POOL_WORK.split()[i], k, odd, scan, proj, tail, moe)
                assert done == {"c": NS, "i": NS, "m": len(POOL_WORK.split()), "a": NETS}

            run_steps(pool, step)

        @block.scalar
        def _(act):
            act.wait_ge(mixer_weights, MIXER_LOADED)
            act.activation(A_sb[:], chan_sb[:, :, 0:NS], ACT.Exp).then_inc(a_exp, 1)
            act.wait_ge(a_exp, 1)
            act.activation(A_sb[:], A_sb[:], ACT.Copy, scale=-1.0).then_inc(a_ready, 1)
            for j in range(TAP_USES):
                act.wait_ge(tap_in_psum, j + 1)
                act.activation(wtap_s[0][:, 2 * j:2 * j + 2], p_misc[:].rearrange("p (k c) -> p k c", k=2),
                               ACT.Copy).then_inc(tap_hi, 1)
            for w, (hi, lo) in mixer_splits:
                act.activation(hi[:], w[:], ACT.Copy).then_inc(mixer_hi, 1)
            act.wait_ge(a_ready, 1)
            act.wait_ge(consts, CONSTS)

            def add_eps(g, n):
                j = NS * g + n
                act.wait_ge(input_done, j + 1)
                act.activation(dB[:, n % DB_RING], dB[:, n % DB_RING], ACT.Copy, bias=STATE_EPS
                               ).then_inc(eps_added, 1)

            def decays(g, n):
                if n == 0:
                    act.wait_ge(dt_ready, g + 1)
                    act.wait_ge(starts_zeroed, 1)
                j = NS * g + n
                at_least(act, scan_done, j - DA_RING + 1)
                for half in range(HALVES):
                    src = dt_sb[:, half].rearrange("p (s t) -> p s t", s=SPG)
                    dst = dA[:, n % DA_RING, half].rearrange("p (s t) -> p s t", s=SPG)
                    act.activation(dst[:, :, 1:], src[:, :, 1:], ACT.Exp,
                                   scale=A_sb[:, half, n:n + 1]).then_inc(exp_done, 1)

            def misc_work(kind, k, odd, scan, proj, tail, moe):
                G, M = k + 1, k - 1
                if kind == "xnT" and proj:
                    act.wait_ge(xnT_in_psum, G + 1)
                    at_least(act, z_in_psum, 2 * G)
                    act.activation(xnT_s[0][:, :, TAPS - 1:], p_misc[:].rearrange("p (s t) -> p s t", s=SPG),
                                   ACT.Copy).then_inc(xnT_hi_ready, 1)
                if kind in ("u0", "u1") and proj:
                    half = int(kind[1])
                    act.wait_ge(u_in_psum, 2 * G + half + 1)
                    if tail:
                        act.wait_ge(yd_ready, 2 * M + half + 1)
                    act.activation(u_sb[:, 1 - odd, half], p_misc[:], ACT.Identity,
                                   bias=chan_sb[:, half, NS:NS + 1])
                    at_least(act, bc_in_psum, G)
                    act.activation(u_s[0][:, half], p_misc[:], ACT.Identity,
                                   bias=chan_sb[:, half, NS:NS + 1]).then_inc(u_ready, 1)
                if kind in ("u0", "u1") and proj and not scan:
                    act.wait_ge(expert_weights, EXPERTS_LOADED)
                    w, (hi, lo) = expert_splits[int(kind[1])]
                    act.activation(hi[:], w[:], ACT.Copy).then_inc(expert_hi, 1)
                if kind == "xn2T" and tail:
                    act.wait_ge(xn2T_in_psum, M + 1)
                    at_least(act, up_in_psum, UNITS * (M - 1))
                    act.activation(xn2T_s[1 - odd][0][:], p_misc[:], ACT.Copy).then_inc(xn2T_hi_ready, 1)
                if kind in ("dt0", "dt1") and proj:
                    half = int(kind[2])
                    act.wait_ge(dtl_in_psum, 2 * G + half + 1)
                    act.activation(dtl[:, half], p_misc[:], ACT.Identity,
                                   bias=chan_sb[:, half, NS + 1:NS + 2]).then_inc(dtl_ready, 1)
                if kind in ("z0", "z1") and proj:
                    half = int(kind[1])
                    act.wait_ge(z_in_psum, 2 * G + half + 1)
                    if tail:
                        act.wait_ge(yz_ready, 2 * (M + 1))
                    act.activation(sz[:, 1 - odd, half], p_misc[:], ACT.Silu).then_inc(sz_ready, 1)
                if kind == "logit" and tail:
                    act.wait_ge(logit_in_psum, M + 1)
                    act.activation(logit[:], p_misc[:, 0:CHUNKS * EXPERTS].rearrange(
                        "p (c e) -> p c e", c=CHUNKS), ACT.Copy).then_inc(logit_ready, 1)
                if kind == "bc" and proj:
                    act.wait_ge(bc_in_psum, G + 1)
                    act.activation(bc_sb, p_misc[0:2 * NS], ACT.Copy).then_inc(bc_ready, 1)
                if kind == "c" and proj:
                    act.wait_ge(c_in_psum, G + 1)
                    if tail:
                        act.wait_ge(mac_done, PAIRS * NS * k)
                    act.activation(c_sb[:, 1 - odd], p_misc[:, 0:CHUNKS * 2 * NS].rearrange(
                        "p (c n) -> p c n", c=CHUNKS)[:, :, NS:], ACT.Copy).then_inc(c_ready, 1)
                if kind == "sigmoid_dt" and proj:
                    act.wait_ge(dtl_ready, 2 * (G + 1))
                    if scan:
                        act.wait_ge(exp_done, 2 * NS * G)
                    act.activation(dt_sb[:], dtl[:], ACT.Sigmoid).then_inc(dt_raw, 1)
                if kind == "sigmoid_router" and tail:
                    act.wait_ge(logit_ready, M + 1)
                    at_least(act, route_ready, M)
                    act.activation(prob[:], logit[:], ACT.Sigmoid).then_inc(prob_ready, 1)

            def scale_net(Q, e, odd):
                act.wait_ge(down_in_psum, NETS * Q + e + 1)
                act.wait_ge(route_ready, Q + 1)
                if pool_nets.index(e) < 2:
                    at_least(act, net_added, NETS * (Q - 1) + pool_nets[pool_nets.index(e) - 2] + 1)
                else:
                    at_least(act, net_added, NETS * Q + pool_nets[pool_nets.index(e) - 2] + 1)
                for c in range(CHUNKS):
                    op = act.activation(scaled[:, pool_nets.index(e) % 2, c], p_down[:, c], ACT.Identity,
                                        scale=route[:, odd, c, e - 1:e])
                op.then_inc(net_scaled, 1)

            def silu(Q, i):
                act.wait_ge(gate_in_psum, UNITS * Q + i + 1)
                at_least(act, down_in_psum, NETS * Q + i // 2 - HM_RING + 1)
                act.activation(hm[:, i // 2 % HM_RING, i % 2], p_gate[i % 2][:], ACT.Silu).then_inc(silu_done, 1)

            def step(k, odd, scan, proj, tail, moe):
                done = {kind: 0 for kind in "exgmd"}
                for kind in ACT_ORDER.replace(" ", ""):
                    i = done[kind]
                    done[kind] += 1
                    lead = {"e": EPS_LEAD, "x": DECAY_LEAD}
                    if kind in "ex":
                        n = i + lead[kind]
                        work = add_eps if kind == "e" else decays
                        if n < NS and scan:
                            work(k, n)
                        if n >= NS and proj:
                            work(k + 1, n - NS)
                    if kind == "g" and moe:
                        silu(k - 2, i)
                    if kind == "d" and moe and i in pool_nets:
                        scale_net(k - 2, i, odd)
                    if kind == "m":
                        misc_work(ACT_WORK.split()[i], k, odd, scan, proj, tail, moe)
                assert done == {"e": NS, "x": NS, "g": UNITS, "m": len(ACT_WORK.split()), "d": NETS}

            run_steps(act, step)

        @block.tensor
        def _(pe):
            pe.wait_ge(tap_weights, 16 * len(tap_loads))
            for j in range(TAP_USES):
                at_least(pe, tap_split, j)
                for q in range(2):
                    for half in range(HALVES):
                        mm = pe.matmul(p_misc[:, q * CH:(q + 1) * CH], win_sb[:, half],
                                       wconv_sb[:, half, 2 * j + q],
                                       start=half == 0, stop=half == HALVES - 1)
                mm.then_inc(tap_in_psum, 1)
            pe.wait_ge(mixer_weights, MIXER_LOADED)
            pe.wait_ge(ident_set, 2)
            pe.wait_ge(consts, CONSTS)
            pe.wait_ge(tap_split, TAP_USES)
            pe.wait_ge(amin_ready, 1)
            pe.matmul(p_down[0:1, 0], amin[:], ident[:], start=True, stop=True).then_inc(amin_in_psum, 1)

            def states_by_token(g, n):
                j = NS * g + n
                pe.wait_ge(scan_done, j + 1)
                for pair in range(PAIRS):
                    at_least(pe, mac_done, PAIRS * (j - 1) + pair + 1)
                    for c in range(2):
                        for half in range(HALVES):
                            t0 = (2 * pair + c) * P
                            mm = pe.transpose(p_hT[pair][:, c, half * P:(half + 1) * P],
                                              h[:, n % 2, half, t0:t0 + P], ident[:])
                    mm.then_inc(hT_in_psum, 1)

            def split_matmul(out, w, x, start, stop):
                pe.matmul(out, w[0], x[0], start=start, stop=False)
                pe.matmul(out, w[0], x[1], start=False, stop=False)
                return pe.matmul(out, w[1], x[0], start=False, stop=stop)

            def both(parts, *index):
                return tuple(p[index] for p in parts)

            def use_yback(M, half, odd, last):
                pe.wait_ge(mac_done, PAIRS * NS * (M + 1))
                if half == 1:
                    pe.wait_ge(yd_ready, 2 * M + 1)
                elif last:
                    pe.wait_ge(logit_ready, M)
                else:
                    pe.wait_ge(c_ready, M + 2)
                for c in range(CHUNKS):
                    mm = pe.transpose(p_misc[:, c * P:(c + 1) * P],
                                      yT[:, c, half * P:(half + 1) * P], ident[:])
                mm.then_inc(yb_in_psum, 1)

            def use_xnT(G, tail):
                pe.wait_ge(xn_ready, G + 1)
                if tail:
                    pe.wait_ge(yd_ready, 2 * (G - 1))
                else:
                    at_least(pe, c_ready, G)
                for c in range(CHUNKS):
                    mm = pe.transpose(p_misc[:, c * P:(c + 1) * P], xn[:, c], ident[:])
                mm.then_inc(xnT_in_psum, 1)

            def use_outproj(M, proj):
                pe.wait_ge(yz_ready, 2 * (M + 1))
                if proj:
                    pe.wait_ge(xnT_ready, M + 3)
                for c in range(CHUNKS):
                    for half in range(HALVES):
                        mm = pe.matmul(p_misc[:, c * DM:(c + 1) * DM], yz[:, half, c * P:(c + 1) * P],
                                       wout_sb[:, half], start=half == 0, stop=half == HALVES - 1)
                mm.then_inc(op_in_psum, 1)

            def use_u(G, half, tail):
                pe.wait_ge(xnT_ready, G + 1)
                if half == 1:
                    pe.wait_ge(u_ready, 2 * G + 1)
                elif tail:
                    pe.wait_ge(x1_ready, G - 1)
                for t in range(TAPS):
                    mm = split_matmul(p_misc[:].rearrange("p (s t) -> p s t", s=SPG),
                                      both(wtap_s, ALL, t, slice(half * P, (half + 1) * P)),
                                      both(xnT_s, ALL, ALL, slice(t, t + SEQ)),
                                      t == 0, t == TAPS - 1)
                mm.then_inc(u_in_psum, 1)

            def use_xn2T(M, proj):
                pe.wait_ge(xn2_ready, M + 1)
                if proj:
                    pe.wait_ge(u_ready, 2 * (M + 3))
                for c in range(CHUNKS):
                    mm = pe.transpose(p_misc[:, c * P:(c + 1) * P], xn2[:, c], ident[:])
                mm.then_inc(xn2T_in_psum, 1)

            def use_dt(G, half, tail):
                pe.wait_ge(u_split, 2 * (G + 1))
                if half == 1:
                    pe.wait_ge(dtl_ready, 2 * G + 1)
                elif tail:
                    pe.wait_ge(xn2T_ready, G - 1)
                for q in range(HALVES):
                    mm = split_matmul(p_misc[:], both(wdt_s, ALL, q, slice(half * P, (half + 1) * P)),
                                      both(u_s, ALL, q), q == 0, q == HALVES - 1)
                mm.then_inc(dtl_in_psum, 1)

            def use_logit(M, odd, proj):
                pe.wait_ge(xn2T_ready, M + 1)
                if proj:
                    pe.wait_ge(sz_ready, 2 * (M + 2) + 1)
                for c in range(CHUNKS):
                    o = p_misc[:, c * EXPERTS:(c + 1) * EXPERTS]
                    split_matmul(o, both(xn2T_s[odd], ALL, slice(c * P, (c + 1) * P)),
                                 both(wr_s, ALL, ALL), True, False)
                    mm = pe.matmul(o, ones[:], br_sb[:], start=False, stop=True)
                mm.then_inc(logit_in_psum, 1)

            def use_bc(G):
                pe.wait_ge(sz_ready, 2 * (G + 1))
                for q in range(HALVES):
                    mm = split_matmul(p_misc[0:2 * NS], both(wbc_s, ALL, q, ALL),
                                      both(u_s, ALL, q), q == 0, q == HALVES - 1)
                mm.then_inc(bc_in_psum, 1)

            def use_c(G):
                pe.wait_ge(bc_ready, G + 1)
                for c in range(CHUNKS):
                    mm = pe.matmul(p_misc[:, c * 2 * NS:(c + 1) * 2 * NS], bc_sb[:, c * P:(c + 1) * P],
                                   ident[0:2 * NS, 0:2 * NS], start=True, stop=True)
                mm.then_inc(c_in_psum, 1)

            def use_z(G, half, tail):
                if half == 0:
                    pe.wait_ge(dtl_ready, 2 * (G + 1))
                elif tail:
                    pe.wait_ge(logit_ready, G - 1)
                else:
                    pe.wait_ge(sz_ready, 2 * G + 1)
                split_matmul(p_misc[:].rearrange("p (s t) -> p s t", s=SPG),
                             both(wz_s, ALL, slice(half * P, (half + 1) * P)),
                             both(xnT_s, ALL, ALL, slice(TAPS - 1, None)),
                             True, True).then_inc(z_in_psum, 1)

            def gate_up(M, i, odd):
                e, half = divmod(i, 2)
                part = ALL, e, slice(half * P, (half + 1) * P)
                if i == 0:
                    pe.wait_ge(xn2T_ready, M + 1)
                at_least(pe, silu_done, UNITS * M + i - 1)
                split_matmul(p_gate[i % 2][:], both(wg_s, *part), both(xn2T_s[odd], ALL),
                             True, True).then_inc(gate_in_psum, 1)
                at_least(pe, prod_done, UNITS * M + i - 1)
                split_matmul(p_up[i % 2][:], both(wu_s, *part), both(xn2T_s[odd], ALL),
                             True, True).then_inc(up_in_psum, 1)

            def down(M, e, odd):
                pe.wait_ge(prod_done, UNITS * M + 2 * e + 2)
                if e - 1 in pool_nets:
                    pe.wait_ge(net_scaled, len(pool_nets) * M + pool_nets.index(e - 1) + 1)
                elif e == 0 and NETS - 1 in pool_nets:
                    at_least(pe, net_scaled, len(pool_nets) * M)
                else:
                    at_least(pe, net_added, NETS * M + e)
                for c in range(CHUNKS):
                    for half in range(2):
                        mm = pe.matmul(p_down[:, c], hm[:, e % HM_RING, half, c * P:(c + 1) * P],
                                       wd_sb[:, e, half], start=half == 0, stop=half == 1)
                mm.then_inc(down_in_psum, 1)

            def use_misc(kind, k, odd, scan, proj, tail, moe):
                G, M = k + 1, k - 1
                if kind in ("yb0", "yb1") and tail:
                    use_yback(M, int(kind[2]), 1 - odd, isinstance(k, int) and k == GROUPS)
                if kind == "xnT" and proj:
                    use_xnT(G, tail)
                if kind == "op" and tail:
                    use_outproj(M, proj)
                if kind in ("u0", "u1") and proj:
                    use_u(G, int(kind[1]), tail)
                if kind == "xn2T" and tail:
                    use_xn2T(M, proj)
                if kind in ("dt0", "dt1") and proj:
                    use_dt(G, int(kind[2]), tail)
                if kind in ("z0", "z1") and proj:
                    use_z(G, int(kind[1]), tail)
                if kind == "logit" and tail:
                    use_logit(M, 1 - odd, proj)
                if kind == "bc" and proj:
                    use_bc(G)
                if kind == "c" and proj:
                    use_c(G)

            def step(k, odd, scan, proj, tail, moe):
                done = {kind: 0 for kind in "hwm"}
                for kind in PE_ORDER.replace(" ", ""):
                    i = done[kind]
                    done[kind] += 1
                    if kind == "h" and scan:
                        states_by_token(k, i)
                    if kind == "w" and moe:
                        item = WORK.split()[i]
                        (gate_up if item[0] == "G" else down)(k - 2, int(item[1:]), odd)
                    if kind == "m":
                        use_misc(MISC_USES.split()[i], k, odd, scan, proj, tail, moe)
                assert done == {"h": NS, "w": UNITS + NETS, "m": len(MISC_USES.split())}

            pe.wait_ge(mixer_split, len(mixer_splits))
            run_steps(pe, step)

        @block.vector
        def _(dve):
            dve.wait_ge(consts, CONSTS)
            dve.wait_ge(a_ready, 1)
            dve.tensor_reduce(amin[:], A_sb[:].rearrange("p h n -> p (h n)"), AX.X, ALU.min).then_inc(amin_ready, 1)
            for j in range(TAP_USES):
                dve.wait_ge(tap_hi, j + 1)
                dve.tensor_tensor(wtap_s[1][:, 2 * j:2 * j + 2], p_misc[:].rearrange("p (k c) -> p k c", k=2),
                                  wtap_s[0][:, 2 * j:2 * j + 2].bitcast(F32),
                                  ALU.subtract).then_inc(tap_split, 1)
            dve.wait_ge(amin_in_psum, 1)
            dve.tensor_reduce(amin_all[:], p_down[0:1, 0], AX.X, ALU.min).then_inc(flag_ready, 1)
            dve.wait_ge(flag_ready, 1)
            dve.tensor_scalar(flag[:], amin_all[:], -CLIP, None, ALU.is_lt).then_inc(flag_ready, 1)
            for j, (w, (hi, lo)) in enumerate(mixer_splits):
                dve.wait_ge(mixer_hi, j + 1)
                dve.tensor_tensor(lo[:], w[:], hi[:].bitcast(F32), ALU.subtract).then_inc(mixer_split, 1)

            def scan_state(g, n):
                j = NS * g + n
                at_least(dve, hT_in_psum, PAIRS * (j - 1))
                dve.wait_ge(eps_added, j + 1)
                dve.wait_ge(clamp_done, j + 1)
                flat = "p h t -> p (h t)"
                dve.tensor_tensor_scan(h[:, n % 2].rearrange(flat), dA[:, n % DA_RING].rearrange(flat),
                                       dB[:, n % DB_RING].rearrange(flat), 0.0,
                                       ALU.mult, ALU.add).then_inc(scan_done, 1)

            def sum_states(g, n, odd):
                j = NS * g + n
                for pair in range(PAIRS):
                    dve.wait_ge(hT_in_psum, PAIRS * j + pair + 1)
                    if n == 0 and pair == 0:
                        dve.wait_ge(c_ready, g + 1)
                        at_least(dve, yb_in_psum, 2 * g)
                    at_least(dve, mac_done, PAIRS * (j - 1) + pair + 1)
                    for c in range(2):
                        cc = 2 * pair + c
                        scalar = c_sb[:, odd, cc, n:n + 1]
                        if n == 0:
                            op = dve.tensor_scalar(yT[:, cc], p_hT[pair][:, c], scalar, None, ALU.mult)
                        else:
                            op = dve.scalar_tensor_tensor(yT[:, cc], p_hT[pair][:, c], scalar,
                                                          yT[:, cc], ALU.mult, ALU.add)
                    op.then_inc(mac_done, 1)

            def norm_stats(g, src, stats, mv, stats_done, mv_done):
                for c in range(CHUNKS):
                    dve.bn_stats(stats[:, c], src[:, c]).then_inc(stats_done, 1)
                wait_apart(dve, stats_done, CHUNKS * (g + 1), dve_passed)
                for c in range(CHUNKS):
                    dve.bn_aggr(mv[:, c], stats[:, c]).then_inc(mv_done, 1)

            def pick_expert(M, j, odd):
                wide = [P, CHUNKS, EXPERTS]
                rank_b = rank[:].rearrange("p (o e) -> p o e", o=1).broadcast_to(wide)

                def spread(v):
                    return v[:].rearrange("p (c o) -> p c o", o=1).broadcast_to(wide)

                count = [0, 6][j]

                def then(op):
                    nonlocal count
                    count += 1
                    op.then_inc(route_step, 1)
                    dve.wait_ge(route_step, ROUTE_STEPS * M + count)

                src = (prob, rest)[j]
                if j == 0:
                    dve.wait_ge(prob_ready, M + 1)
                then(dve.tensor_reduce(top[j][:], src[:], AX.X, ALU.max))
                then(dve.tensor_tensor(key[:], src[:], spread(top[j]), ALU.is_equal))
                then(dve.tensor_tensor(key[:], key[:], rank_b, ALU.mult))
                then(dve.tensor_reduce(win[:], key[:], AX.X, ALU.max))
                then(dve.tensor_tensor(hit[j][:], key[:], spread(win), ALU.is_equal))
                if j == 0:
                    then(dve.scalar_tensor_tensor(rest[:], hit[0][:], -2.0, prob[:], ALU.mult, ALU.add))
                    return
                then(dve.tensor_tensor(win[:], top[0][:], top[1][:], ALU.add))
                then(dve.reciprocal(share[:], win[:]))
                then(dve.tensor_tensor(key[:], hit[0][:], hit[1][:], ALU.add))
                then(dve.tensor_tensor(key[:], key[:], spread(share), ALU.mult))
                assert count == ROUTE_STEPS
                dve.tensor_tensor(route[:, odd], key[:], prob[:], ALU.mult).then_inc(route_ready, 1)

            def product(M, i):
                e, half = divmod(i, 2)
                dve.wait_ge(silu_done, UNITS * M + i + 1)
                dve.wait_ge(up_in_psum, UNITS * M + i + 1)
                dve.tensor_tensor(hm[:, e % HM_RING, half], p_up[i % 2][:], hm[:, e % HM_RING, half], ALU.mult).then_inc(prod_done, 1)

            def add_net(M, e, odd):
                dve.wait_ge(down_in_psum, NETS * M + e + 1)
                at_least(dve, net_added, NETS * M + e)
                if e == 0:
                    dve.tensor_tensor(x1[:, odd], p_down[:], x1[:, odd], ALU.add).then_inc(net_added, 1)
                    return
                if e == min(set(range(1, NETS)) - set(pool_nets)):
                    dve.wait_ge(route_ready, M + 1)
                for c in range(CHUNKS):
                    op = dve.scalar_tensor_tensor(x1[:, odd, c], p_down[:, c], route[:, odd, c, e - 1:e],
                                                  x1[:, odd, c], ALU.mult, ALU.add)
                op.then_inc(net_added, 1)

            def norm_apply(dst, src, mv, rs, done):
                for c in range(CHUNKS):
                    op = dve.tensor_scalar(dst[:, c], src[:, c], mv[:, c, 0:1], rs[:, c:c + 1],
                                           ALU.subtract, ALU.mult)
                op.then_inc(done, 1)

            def other_work(kind, k, odd, scan, proj, tail, moe):
                G, M = k + 1, k - 1
                if kind == "stats1" and proj:
                    dve.wait_ge(x_loaded[1 - odd], transfers(G, 1 - odd))
                    at_least(dve, xn_ready, G)
                    norm_stats(G, x_sb[:, 1 - odd], stats, mv1, ln1_stats, ln1_mv)
                if kind == "xn" and proj:
                    dve.wait_ge(ln1_rstd, G + 1)
                    at_least(dve, c_in_psum, G)
                    at_least(dve, b_stored, 16 * G)
                    norm_apply(xn, x_sb[:, 1 - odd], mv1, rstd1, xn_ready)
                if kind in ("yd0", "yd1") and tail:
                    half = int(kind[2])
                    dve.wait_ge(yb_in_psum, 2 * M + half + 1)
                    at_least(dve, yz_ready, 2 * M)
                    dve.scalar_tensor_tensor(yz[:, half], u_sb[:, 1 - odd, half],
                                             chan_sb[:, half, NS + 2:NS + 3], p_misc[:],
                                             ALU.mult, ALU.add).then_inc(yd_ready, 1)
                if kind == "xnT_lo" and proj:
                    dve.wait_ge(xnT_hi_ready, G + 1)
                    dve.tensor_tensor(xnT_s[1][:, :, TAPS - 1:], p_misc[:].rearrange("p (s t) -> p s t", s=SPG),
                                      xnT_s[0][:, :, TAPS - 1:].bitcast(F32),
                                      ALU.subtract).then_inc(xnT_ready, 1)
                if kind == "x1" and proj and not scan:
                    for j, (w, (hi, lo)) in enumerate(expert_splits):
                        dve.wait_ge(expert_hi, j + 1)
                        dve.tensor_tensor(lo[:], w[:], hi[:].bitcast(F32), ALU.subtract).then_inc(expert_split, 1)
                if kind == "x1" and tail:
                    dve.wait_ge(op_in_psum, M + 1)
                    dve.wait_ge(res_loaded, 16 * (M + 1))
                    at_least(dve, out_stored[1 - odd], transfers(M, 1 - odd) - 16)
                    dve.tensor_tensor(x1[:, 1 - odd], p_misc[:].rearrange("p (c d) -> p c d", c=CHUNKS),
                                      res[:], ALU.add).then_inc(x1_ready, 1)
                if kind == "stats2" and tail:
                    dve.wait_ge(x1_ready, M + 1)
                    at_least(dve, xn2_ready, M)
                    norm_stats(M, x1[:, 1 - odd], stats, mv2, ln2_stats, ln2_mv)
                if kind == "xn2" and tail:
                    dve.wait_ge(ln2_rstd, M + 1)
                    if proj:
                        dve.wait_ge(xnT_in_psum, G + 1)
                    norm_apply(xn2, x1[:, 1 - odd], mv2, rstd2, xn2_ready)
                if kind == "xn2T_lo" and tail:
                    dve.wait_ge(xn2T_hi_ready, M + 1)
                    dve.tensor_tensor(xn2T_s[1 - odd][1][:], p_misc[:], xn2T_s[1 - odd][0][:].bitcast(F32),
                                      ALU.subtract).then_inc(xn2T_ready, 1)
                if kind == "clip_dt" and proj:
                    dve.wait_ge(dt_raw, G + 1)
                    dve.tensor_scalar(dt_sb[:], dt_sb[:], DT_MIN, 1.0, ALU.max, ALU.min).then_inc(dt_ready, 1)
                if kind in ("pick0", "pick1") and tail:
                    pick_expert(M, int(kind[4]), 1 - odd)

            def step(k, odd, scan, proj, tail, moe):
                done = {kind: 0 for kind in "sypam"}
                for kind in DVE_ORDER.replace(" ", ""):
                    i = done[kind]
                    done[kind] += 1
                    if kind == "s" and scan:
                        scan_state(k, i)
                    if kind == "y" and i > 0 and scan:
                        sum_states(k, i - 1, odd)
                    if kind == "y" and i == 0 and tail:
                        sum_states(k - 1, NS - 1, 1 - odd)
                    if kind == "p" and moe:
                        product(k - 2, i)
                    if kind == "a" and moe and i not in pool_nets:
                        add_net(k - 2, i, odd)
                    if kind == "m":
                        other_work(DVE_WORK.split()[i], k, odd, scan, proj, tail, moe)
                assert done == {"s": NS, "y": NS, "p": UNITS, "a": NETS, "m": len(DVE_WORK.split())}

            run_steps(dve, step)


_OUT = "out_dram"


def kernel(**inputs):
    import concourse.bacc as bacc
    from concourse.bass_utils import run_bass_kernel_spmd

    a = {n: np.asarray(v) for n, v in inputs.items()}
    x = a["L0_attn_x"]

    def parts(m):
        return m.reshape((m.shape[0] // P, P) + m.shape[1:]).swapaxes(0, 1)

    w_in = a["L0_attn_in_proj_w"]
    gates = np.concatenate([a["L0_ffn_sg_w"][None], a["L0_ffn_wg"]])
    ups = np.concatenate([a["L0_ffn_su_w"][None], a["L0_ffn_wu"]])
    downs = np.concatenate([a["L0_ffn_sd_w"][None], a["L0_ffn_wd"]])
    arrays = {
        "x": x.reshape(TOKENS, DM),
        "w_in": parts(w_in[:CH]),
        "w_z": w_in[CH:].T,
        "w_conv": parts(a["L0_attn_conv_w"].transpose(1, 2, 0)),
        "w_dt": parts(a["L0_attn_dt_w"].T),
        "w_bc": parts(np.concatenate([a["L0_attn_B_w"], a["L0_attn_C_w"]]).T),
        "w_out": parts(a["L0_attn_out_w"].T),
        "chan": parts(np.concatenate([a["L0_attn_A_log"], a["L0_attn_conv_b"][:, None],
                                      a["L0_attn_dt_b"][:, None], a["L0_attn_D"][:, None]], axis=1)),
        "w_router": a["L0_ffn_router_w"].T,
        "b_router": a["L0_ffn_routing_bias"][None],
        "w_gate": gates.transpose(2, 0, 1),
        "w_up": ups.transpose(2, 0, 1),
        "w_down": downs.transpose(2, 0, 1).reshape(2, P, NETS, DM).transpose(1, 2, 0, 3),
    }
    nc = bacc.Bacc("TRN2", target_bir_lowering=False, num_devices=1)
    feed, args = {}, []
    for name, arr in arrays.items():
        arr = np.ascontiguousarray(arr)
        feed[f"{name}_dram"] = arr
        args.append(nc.dram_tensor(f"{name}_dram", arr.shape, mybir.dt.from_np(arr.dtype),
                                   kind="ExternalInput").ap())
    out = nc.dram_tensor(_OUT, (TOKENS, DM), F32, kind="ExternalOutput").ap()
    b_rows = nc.dram_tensor("b_rows_dram", (2, NS, TOK), F32, kind="Internal").ap()
    build(nc, *args, b_rows, out)
    r = run_bass_kernel_spmd(nc, [feed], core_ids=[0])
    return r.results[0][_OUT].reshape(x.shape)
```
